# Optimizing a Trainium2 kernel written in Bass

```python
import numpy as np
import jax
import jax.numpy as jnp

def _softmax(x, axis=-1):
    return jax.nn.softmax(x, axis=axis)

def _gelu(x):
    return jax.nn.gelu(x, approximate=True)

def _silu(x):
    return jax.nn.silu(x)

def _sigmoid(x):
    return jax.nn.sigmoid(x)

def _layernorm(x, axis=-1, eps=1e-05):
    m = jnp.mean(x, axis=axis, keepdims=True)
    v = jnp.var(x, axis=axis, keepdims=True)
    return (x - m) / jnp.sqrt(v + eps)

def _scatter_add(tgt, idx, src, axis=0):
    return tgt.at[idx].add(src)

def _segment_sum(src, seg, n):
    return jax.ops.segment_sum(src, seg, n)
kernel_name = 'mk_audio_tower_d2_tok_audfeat256_r4_16f496'

def setup_inputs(seed: int=0):
    np.random.seed(seed)
    _w = jnp.asarray

    def _rec_inputs():
        import jax
        import jax.numpy as jnp
        _rk = jax.random.key(seed)
        x = -0.000392918 + 0.999932 * jax.random.normal(jax.random.fold_in(_rk, 1), (64, 375, 16), jnp.float32)
        return x
    x = _rec_inputs()

    def _L0_tok_setup():
        import jax, jax.numpy as jnp
        import numpy as np
        PATCH = 16
        STRIDE = 8
        EPS = 1e-05
        key = jax.random.key(seed)
        k1, k2, k3 = jax.random.split(key, 3)
        B, S, F, D = (128, 2048, 16, 64)
        in_dim = F * PATCH
        x = jax.random.normal(k1, (B, S, F), dtype=jnp.float32)
        bound = 1.0 / np.sqrt(in_dim)
        W = jax.random.uniform(k2, (D, in_dim), minval=-bound, maxval=bound, dtype=jnp.float32)
        b = jax.random.uniform(k3, (D,), minval=-bound, maxval=bound, dtype=jnp.float32)
        gamma = jnp.ones((D,), dtype=jnp.float32)
        beta = jnp.zeros((D,), dtype=jnp.float32)
        return {'x': x, 'W': W, 'b': b, 'gamma': gamma, 'beta': beta}
    _L0_tok_all = _L0_tok_setup()
    _L0_tok_in = {k: v for k, v in _L0_tok_all.items() if k in ('W', 'b', 'gamma', 'beta')}
    del _L0_tok_all

    def _L0_attn_setup():
        import jax, jax.numpy as jnp
        import numpy as np
        BN_EPS = 1e-05
        key = jax.random.key(seed)
        ks = jax.random.split(key, 12)
        B, N, d_e, d_a = (16, 512, 64, 64)
        s_e = 1.0 / np.sqrt(d_e)
        return {'x': jax.random.normal(ks[0], (B, N, d_e), dtype=jnp.float32), 'Wq': jax.random.uniform(ks[1], (d_e, d_a), jnp.float32, -s_e, s_e), 'bq': jax.random.uniform(ks[2], (d_a,), jnp.float32, -s_e, s_e), 'Wk': jax.random.uniform(ks[3], (d_e, d_a), jnp.float32, -s_e, s_e), 'bk': jax.random.uniform(ks[4], (d_a,), jnp.float32, -s_e, s_e), 'Wv': jax.random.uniform(ks[5], (d_e, d_e), jnp.float32, -s_e, s_e), 'bv': jax.random.uniform(ks[6], (d_e,), jnp.float32, -s_e, s_e), 'Wl': jax.random.uniform(ks[7], (d_e, d_e), jnp.float32, -s_e, s_e), 'bl': jax.random.uniform(ks[8], (d_e,), jnp.float32, -s_e, s_e), 'gamma': jnp.ones((d_e,), jnp.float32), 'beta': jnp.zeros((d_e,), jnp.float32)}
    _L0_attn_all = _L0_attn_setup()
    _L0_attn_in = {k: v for k, v in _L0_attn_all.items() if k in ('Wq', 'bq', 'Wk', 'bk', 'Wv', 'bv', 'Wl', 'bl', 'gamma', 'beta')}
    del _L0_attn_all

    def _L0_ffn_setup():
        import jax, jax.numpy as jnp
        import numpy as np
        B, K, D = (128, 16, 64)
        E = 32
        H = int(D * 0.25)
        key = jax.random.key(seed)
        ks = jax.random.split(key, 7)
        d_rs = D ** (-0.5)
        h_rs = H ** (-0.5)
        x = jax.random.normal(ks[0], (B, K, D), dtype=jnp.float32)
        router_w = jax.random.uniform(ks[1], (E, D), jnp.float32, -d_rs, d_rs)
        router_b = jax.random.uniform(ks[2], (E,), jnp.float32, -d_rs, d_rs)
        W1 = jax.random.uniform(ks[3], (E, D, H), jnp.float32, -h_rs, h_rs)
        b1 = jax.random.uniform(ks[4], (E, H), jnp.float32, -h_rs, h_rs)
        W2 = jax.random.uniform(ks[5], (E, H, D), jnp.float32, -d_rs, d_rs)
        b2 = jax.random.uniform(ks[6], (E, D), jnp.float32, -d_rs, d_rs)
        return {'x': x, 'router_w': router_w, 'router_b': router_b, 'W1': W1, 'b1': b1, 'W2': W2, 'b2': b2}
    _L0_ffn_all = _L0_ffn_setup()
    _L0_ffn_in = {k: v for k, v in _L0_ffn_all.items() if k in ('router_w', 'router_b', 'W1', 'b1', 'W2', 'b2')}
    del _L0_ffn_all

    def _L1_attn_setup():
        import jax, jax.numpy as jnp
        import numpy as np
        import math
        PI = math.pi

        def _encode_phase(x, w1, b1, w2, b2):
            h = jnp.tanh(jnp.einsum('bld,ed->ble', x, w1) + b1)
            return jnp.tanh(jnp.einsum('bld,kd->blk', h, w2) + b2) * PI
        key = jax.random.key(seed)
        ks = jax.random.split(key, 12)
        B, L, D, K = (2, 512, 64, 32)
        s = 0.02
        return {'x': jax.random.normal(ks[0], (B, L, D), dtype=jnp.float32), 'kw1': jax.random.normal(ks[1], (D, D), dtype=jnp.float32) * s, 'kb1': jnp.zeros((D,), dtype=jnp.float32), 'kw2': jax.random.normal(ks[2], (K, D), dtype=jnp.float32) * s, 'kb2': jnp.zeros((K,), dtype=jnp.float32), 'qw1': jax.random.normal(ks[3], (D, D), dtype=jnp.float32) * s, 'qb1': jnp.zeros((D,), dtype=jnp.float32), 'qw2': jax.random.normal(ks[4], (K, D), dtype=jnp.float32) * s, 'qb2': jnp.zeros((K,), dtype=jnp.float32), 'vw': jax.random.normal(ks[5], (D, D), dtype=jnp.float32) * s, 'vb': jnp.zeros((D,), dtype=jnp.float32)}
    _L1_attn_all = _L1_attn_setup()
    _L1_attn_in = {k: v for k, v in _L1_attn_all.items() if k in ('kw1', 'kb1', 'kw2', 'kb2', 'qw1', 'qb1', 'qw2', 'qb2', 'vw', 'vb')}
    del _L1_attn_all

    def _L1_ffn_setup():
        import jax, jax.numpy as jnp
        import numpy as np
        B, A = (1024, 8)
        IN, OUT = (64, 64)
        SH1, SH2 = (64, 128)
        EH1, EH2 = (128, 64)
        E, TOPK = (4, 2)

        def _shared_mlp(x, W1, b1, W2, b2, W3, b3):
            h = jax.nn.relu(x @ W1 + b1)
            h = jax.nn.relu(h @ W2 + b2)
            return h @ W3 + b3

        def _experts_mlp(x, eW1, eb1, eW2, eb2, eW3, eb3):
            h = jax.nn.relu(jnp.einsum('baf,efh->ebah', x, eW1) + eb1[:, None, None, :])
            h = jax.nn.relu(jnp.einsum('ebah,ehg->ebag', h, eW2) + eb2[:, None, None, :])
            o = jnp.einsum('ebag,ego->ebao', h, eW3) + eb3[:, None, None, :]
            return jnp.moveaxis(o, 0, -1)
        key = jax.random.key(seed)
        ks = jax.random.split(key, 16)
        s = 0.05
        return {'x': jax.random.normal(ks[0], (B, A, IN), jnp.float32), 'sW1': jax.random.normal(ks[1], (IN, SH1), jnp.float32) * s, 'sb1': jnp.zeros((SH1,), jnp.float32), 'sW2': jax.random.normal(ks[2], (SH1, SH2), jnp.float32) * s, 'sb2': jnp.zeros((SH2,), jnp.float32), 'sW3': jax.random.normal(ks[3], (SH2, OUT), jnp.float32) * s, 'sb3': jnp.zeros((OUT,), jnp.float32), 'eW1': jax.random.normal(ks[4], (E, IN, EH1), jnp.float32) * s, 'eb1': jnp.zeros((E, EH1), jnp.float32), 'eW2': jax.random.normal(ks[5], (E, EH1, EH2), jnp.float32) * s, 'eb2': jnp.zeros((E, EH2), jnp.float32), 'eW3': jax.random.normal(ks[6], (E, EH2, OUT), jnp.float32) * s, 'eb3': jnp.zeros((E, OUT), jnp.float32), 'gW': jax.random.normal(ks[7], (IN, E), jnp.float32) * s, 'gb': jnp.zeros((E,), jnp.float32)}
    _L1_ffn_all = _L1_ffn_setup()
    _L1_ffn_in = {k: v for k, v in _L1_ffn_all.items() if k in ('sW1', 'sb1', 'sW2', 'sb2', 'sW3', 'sb3', 'eW1', 'eb1', 'eW2', 'eb2', 'eW3', 'eb3', 'gW', 'gb')}
    del _L1_ffn_all
    return {'x': x, 'L0_tok_W': _L0_tok_in['W'], 'L0_tok_b': _L0_tok_in['b'], 'L0_tok_gamma': _L0_tok_in['gamma'], 'L0_tok_beta': _L0_tok_in['beta'], 'L0_attn_Wq': _L0_attn_in['Wq'], 'L0_attn_bq': _L0_attn_in['bq'], 'L0_attn_Wk': _L0_attn_in['Wk'], 'L0_attn_bk': _L0_attn_in['bk'], 'L0_attn_Wv': _L0_attn_in['Wv'], 'L0_attn_bv': _L0_attn_in['bv'], 'L0_attn_Wl': _L0_attn_in['Wl'], 'L0_attn_bl': _L0_attn_in['bl'], 'L0_attn_gamma': _L0_attn_in['gamma'], 'L0_attn_beta': _L0_attn_in['beta'], 'L0_ffn_router_w': _L0_ffn_in['router_w'], 'L0_ffn_router_b': _L0_ffn_in['router_b'], 'L0_ffn_W1': _L0_ffn_in['W1'], 'L0_ffn_b1': _L0_ffn_in['b1'], 'L0_ffn_W2': _L0_ffn_in['W2'], 'L0_ffn_b2': _L0_ffn_in['b2'], 'L1_attn_kw1': _L1_attn_in['kw1'], 'L1_attn_kb1': _L1_attn_in['kb1'], 'L1_attn_kw2': _L1_attn_in['kw2'], 'L1_attn_kb2': _L1_attn_in['kb2'], 'L1_attn_qw1': _L1_attn_in['qw1'], 'L1_attn_qb1': _L1_attn_in['qb1'], 'L1_attn_qw2': _L1_attn_in['qw2'], 'L1_attn_qb2': _L1_attn_in['qb2'], 'L1_attn_vw': _L1_attn_in['vw'], 'L1_attn_vb': _L1_attn_in['vb'], 'L1_ffn_sW1': _L1_ffn_in['sW1'], 'L1_ffn_sb1': _L1_ffn_in['sb1'], 'L1_ffn_sW2': _L1_ffn_in['sW2'], 'L1_ffn_sb2': _L1_ffn_in['sb2'], 'L1_ffn_sW3': _L1_ffn_in['sW3'], 'L1_ffn_sb3': _L1_ffn_in['sb3'], 'L1_ffn_eW1': _L1_ffn_in['eW1'], 'L1_ffn_eb1': _L1_ffn_in['eb1'], 'L1_ffn_eW2': _L1_ffn_in['eW2'], 'L1_ffn_eb2': _L1_ffn_in['eb2'], 'L1_ffn_eW3': _L1_ffn_in['eW3'], 'L1_ffn_eb3': _L1_ffn_in['eb3'], 'L1_ffn_gW': _L1_ffn_in['gW'], 'L1_ffn_gb': _L1_ffn_in['gb']}

def reference(x, L0_tok_W, L0_tok_b, L0_tok_gamma, L0_tok_beta, L0_attn_Wq, L0_attn_bq, L0_attn_Wk, L0_attn_bk, L0_attn_Wv, L0_attn_bv, L0_attn_Wl, L0_attn_bl, L0_attn_gamma, L0_attn_beta, L0_ffn_router_w, L0_ffn_router_b, L0_ffn_W1, L0_ffn_b1, L0_ffn_W2, L0_ffn_b2, L1_attn_kw1, L1_attn_kb1, L1_attn_kw2, L1_attn_kb2, L1_attn_qw1, L1_attn_qb1, L1_attn_qw2, L1_attn_qb2, L1_attn_vw, L1_attn_vb, L1_ffn_sW1, L1_ffn_sb1, L1_ffn_sW2, L1_ffn_sb2, L1_ffn_sW3, L1_ffn_sb3, L1_ffn_eW1, L1_ffn_eb1, L1_ffn_eW2, L1_ffn_eb2, L1_ffn_eW3, L1_ffn_eb3, L1_ffn_gW, L1_ffn_gb):
    import jax
    import jax.numpy as jnp

    def _L0_tok_ref(x, W, b, gamma, beta):
        import jax, jax.numpy as jnp
        import numpy as np
        PATCH = 16
        STRIDE = 8
        EPS = 1e-05
        B, S, F = x.shape
        starts = jnp.arange(0, S - PATCH + 1, STRIDE)
        idx = starts[:, None] + jnp.arange(PATCH)[None, :]
        patches = x[:, idx, :].reshape(B, idx.shape[0], PATCH * F)
        y = jnp.einsum('bpi,di->bpd', patches, W) + b
        mu = jnp.mean(y, axis=-1, keepdims=True)
        var = jnp.mean(jnp.square(y - mu), axis=-1, keepdims=True)
        return (y - mu) * jax.lax.rsqrt(var + EPS) * gamma + beta

    def _L0_attn_ref(x, Wq, bq, Wk, bk, Wv, bv, Wl, bl, gamma, beta):
        import jax, jax.numpy as jnp
        import numpy as np
        BN_EPS = 1e-05
        q = x @ Wq + bq
        k = x @ Wk + bk
        v = x @ Wv + bv
        d_a = q.shape[-1]
        score = jnp.einsum('bnd,bmd->bnm', q, k) / jnp.asarray(d_a, q.dtype)
        score = jax.nn.softmax(score, axis=2)
        attn = jnp.einsum('bnm,bmd->bnd', score, v)
        h = attn @ Wl + bl
        mean = jnp.mean(h, axis=(0, 1))
        var = jnp.mean((h - mean) ** 2, axis=(0, 1))
        y = jax.nn.relu((h - mean) * jax.lax.rsqrt(var + BN_EPS) * gamma + beta)
        return y + x

    def _L0_ffn_ref(x, router_w, router_b, W1, b1, W2, b2):
        import jax, jax.numpy as jnp
        import numpy as np
        B, K, D = (128, 16, 64)
        E = 32
        H = int(D * 0.25)
        xf = x.reshape(-1, D)
        logits = xf @ router_w.T + router_b
        idx = jnp.argmax(logits, axis=-1)
        w1t = jnp.take(W1, idx, axis=0)
        h = jnp.einsum('nd,ndh->nh', xf, w1t) + jnp.take(b1, idx, axis=0)
        h = jax.nn.relu(h)
        w2t = jnp.take(W2, idx, axis=0)
        out = jnp.einsum('nh,nhd->nd', h, w2t) + jnp.take(b2, idx, axis=0)
        out = jax.nn.relu(out)
        return out.reshape(x.shape)

    def _L1_attn_ref(x, kw1, kb1, kw2, kb2, qw1, qb1, qw2, qb2, vw, vb):
        import jax, jax.numpy as jnp
        import numpy as np
        import math
        PI = math.pi

        def _encode_phase(x, w1, b1, w2, b2):
            h = jnp.tanh(jnp.einsum('bld,ed->ble', x, w1) + b1)
            return jnp.tanh(jnp.einsum('bld,kd->blk', h, w2) + b2) * PI
        B, L, D = x.shape
        key_phase = _encode_phase(x, kw1, kb1, kw2, kb2)
        query_phase = _encode_phase(x, qw1, qb1, qw2, qb2)
        K = key_phase.shape[-1]
        value = jnp.einsum('bld,ed->ble', x, vw) + vb
        cos_k = jnp.cos(key_phase)[..., None]
        sin_k = jnp.sin(key_phase)[..., None]
        v_exp = value[:, :, None, :]
        mem_real = jnp.cumsum(cos_k * v_exp, axis=1)
        mem_imag = jnp.cumsum(sin_k * v_exp, axis=1)
        cos_q = jnp.cos(query_phase)[..., None]
        sin_q = jnp.sin(query_phase)[..., None]
        retrieved = jnp.sum(mem_real * cos_q + mem_imag * sin_q, axis=2)
        positions = jnp.arange(1, L + 1, dtype=x.dtype)
        norm = jnp.sqrt(positions * K)[None, :, None]
        return retrieved / norm

    def _L1_ffn_ref(x, sW1, sb1, sW2, sb2, sW3, sb3, eW1, eb1, eW2, eb2, eW3, eb3, gW, gb):
        import jax, jax.numpy as jnp
        import numpy as np
        B, A = (1024, 8)
        IN, OUT = (64, 64)
        SH1, SH2 = (64, 128)
        EH1, EH2 = (128, 64)
        E, TOPK = (4, 2)

        def _shared_mlp(x, W1, b1, W2, b2, W3, b3):
            h = jax.nn.relu(x @ W1 + b1)
            h = jax.nn.relu(h @ W2 + b2)
            return h @ W3 + b3

        def _experts_mlp(x, eW1, eb1, eW2, eb2, eW3, eb3):
            h = jax.nn.relu(jnp.einsum('baf,efh->ebah', x, eW1) + eb1[:, None, None, :])
            h = jax.nn.relu(jnp.einsum('ebah,ehg->ebag', h, eW2) + eb2[:, None, None, :])
            o = jnp.einsum('ebag,ego->ebao', h, eW3) + eb3[:, None, None, :]
            return jnp.moveaxis(o, 0, -1)
        all_out = _experts_mlp(x, eW1, eb1, eW2, eb2, eW3, eb3)
        shared = _shared_mlp(x, sW1, sb1, sW2, sb2, sW3, sb3)
        gates = jax.nn.softmax(x @ gW + gb, axis=-1)
        topv, topi = jax.lax.top_k(gates, TOPK)
        topw = jax.nn.softmax(topv, axis=-1)
        sel = jnp.take_along_axis(all_out, topi[:, :, None, :], axis=-1)
        gated = jnp.sum(sel * topw[:, :, None, :], axis=-1)
        return shared + gated
    h = _L0_tok_ref(x, L0_tok_W, L0_tok_b, L0_tok_gamma, L0_tok_beta)
    h = h + _L0_attn_ref(_layernorm(h, axis=-1), L0_attn_Wq, L0_attn_bq, L0_attn_Wk, L0_attn_bk, L0_attn_Wv, L0_attn_bv, L0_attn_Wl, L0_attn_bl, L0_attn_gamma, L0_attn_beta)
    h = h + _L0_ffn_ref(_layernorm(h, axis=-1), L0_ffn_router_w, L0_ffn_router_b, L0_ffn_W1, L0_ffn_b1, L0_ffn_W2, L0_ffn_b2)
    h = h + _L1_attn_ref(_layernorm(h, axis=-1), L1_attn_kw1, L1_attn_kb1, L1_attn_kw2, L1_attn_kb2, L1_attn_qw1, L1_attn_qb1, L1_attn_qw2, L1_attn_qb2, L1_attn_vw, L1_attn_vb)
    h = h + _L1_ffn_ref(_layernorm(h, axis=-1), L1_ffn_sW1, L1_ffn_sb1, L1_ffn_sW2, L1_ffn_sb2, L1_ffn_sW3, L1_ffn_sb3, L1_ffn_eW1, L1_ffn_eb1, L1_ffn_eW2, L1_ffn_eb2, L1_ffn_eW3, L1_ffn_eb3, L1_ffn_gW, L1_ffn_gb)
    return h

_drawn_inputs = setup_inputs


def setup_inputs(seed=0):
    import zlib

    import numpy as np

    out = dict(_drawn_inputs(seed))
    spreads = {'L0_tok_gamma': (1.0, 0.2),
     'L0_tok_beta': (0.0, 0.1),
     'L0_attn_gamma': (1.0, 0.2),
     'L0_attn_beta': (0.0, 0.1),
     'L1_attn_kb1': (0.0, 0.8),
     'L1_attn_kb2': (0.0, 0.393),
     'L1_attn_qb1': (0.0, 0.8),
     'L1_attn_qb2': (0.0, 0.1),
     'L1_attn_vb': (0.0, 0.1),
     'L1_ffn_sb1': (0.0, 0.8),
     'L1_ffn_sb2': (0.0, 0.73),
     'L1_ffn_sb3': (0.0, 0.8),
     'L1_ffn_eb1': (0.0, 0.8),
     'L1_ffn_eb2': (0.0, 0.8),
     'L1_ffn_eb3': (0.0, 1.37),
     'L1_ffn_gb': (0.0, 0.8)}
    factors = {'L0_attn_Wq': 3.452,
     'L0_attn_bq': 8.0,
     'L0_attn_Wk': 3.44,
     'L0_attn_bk': 64.0,
     'L0_attn_bv': 64.0,
     'L0_attn_bl': 64.0,
     'L0_ffn_b1': 8.0,
     'L0_ffn_b2': 3.435,
     'L1_attn_kw1': 8.0,
     'L1_attn_kw2': 8.0,
     'L1_attn_qw1': 8.0,
     'L1_attn_qw2': 8.0,
     'L1_ffn_sW1': 6.244,
     'L1_ffn_sW2': 5.419,
     'L1_ffn_sW3': 3.558,
     'L1_ffn_eW1': 7.7,
     'L1_ffn_eW2': 7.319,
     'L1_ffn_eW3': 5.33,
     'L1_ffn_gW': 3.376}
    for name, (base, spread) in spreads.items():
        noise = np.random.default_rng([zlib.crc32(name.encode()), seed]).standard_normal(out[name].shape)
        drawn = base * np.exp(spread * noise) if base else spread * noise
        out[name] = jnp.asarray(drawn.astype(out[name].dtype))
    for name, factor in factors.items():
        out[name] = (out[name] * factor).astype(out[name].dtype)
    return out
```

```python
from contextlib import ExitStack

import numpy as np
import concourse.bass as bass
from concourse import mybir

B, SEQ, FEAT = 64, 375, 16
PATCH, STRIDE, D = 16, 8, 64
TOK = (SEQ - PATCH) // STRIDE + 1
BLOCKS = TOK + PATCH // STRIDE - 1
P = 128
HALVES = P // D
HB = B // HALVES
CHUNKS = 4
CB = HB // CHUNKS
CW = CB * TOK
PADW = CW + D - TOK
TT = 120
NT = CW // TT
NE, NH = 32, 16
MT = NE * NH // P
KP = 32
SH1, SH2, EH1, EH2, EX = 64, 128, 128, 64, 4
BANKS = 8
BIG = 2.0 ** 100
EPS = 1e-5

F32 = mybir.dt.float32
ALU = mybir.AluOpType
ACT = mybir.ActivationFunctionType
AX = mybir.AxisListType

PACK = [
    ("tokW", PATCH * FEAT), ("center", P), ("mean", P), ("tokb", 1), ("tokg", 1), ("tokbeta", 1),
    ("Wq", P), ("Wk", P), ("Wv", P), ("Wl", P), ("bq", 1), ("bk", 1), ("bv", 1), ("bl", 1),
    ("bng", 1), ("bnb", 1), ("avg", P), ("ident", P),
    ("router", HALVES * NE), ("routerb", HALVES * NE), ("rank", HALVES * NE),
    ("W1", HALVES * MT * P), ("M1", HALVES * MT * P), ("W2", MT * D), ("B2", HALVES * D),
    ("kw1", P), ("qw1", P), ("kw2", P), ("qw2", P), ("vw", D), ("vb", CB * D), ("causal", TOK),
    ("kb1", 1), ("qb1", 1), ("kb2", 1), ("qb2", 1), ("fold", 1), ("sscale", 1), ("sbias", 1),
    ("gW", HALVES * EX), ("gb", HALVES * EX), ("grank", HALVES * EX),
    ("sW1", P), ("sW2", HALVES * P), ("sW3", D), ("eW1", HALVES * EX * P), ("eW2", EX * D),
    ("eW3", 2 * D), ("eB3", HALVES * D), ("gsel", HALVES * 2 * P),
    ("sb1", 1), ("sb2", 1), ("sb3", 1), ("eb1", EX), ("eb2", 2),
]
COL, WIDTH = {}, dict(PACK)
_at = 0
for _n, _w in PACK:
    COL[_n] = _at
    _at += _w
PACKW = _at
CUT1 = COL["Wq"]
CUT2 = COL["router"]


def psum_plan():
    tiles = ["setup"]
    each = range(CHUNKS)

    def stage(*names):
        tiles.extend((n, c) for c in each for n in names)

    stage("tok"), stage("var0")
    stage("cen1"), stage("var1")
    stage("q", "k"), stage("va", "vb")
    stage("s"), stage("pta", "ptb"), stage("pv"), stage("wl")
    tiles += ["bn1", "bn2"]
    stage("cen2"), stage("var2")
    stage("lg"), stage("oh")
    for c in range(CHUNKS + 1):
        if c < CHUNKS:
            tiles += [("hid", c, i) for i in range(HALVES * MT)]
        if c:
            tiles.append(("moe", c - 1))
    stage("cen3"), stage("var3")
    stage("k1", "q1"), stage("v3"), stage("k2", "q2")
    stage("st"), stage("ret")
    stage("cen4"), stage("var4")
    tiles.append("gate")
    stage("s1"), stage("s2a", "s2b")
    for c in range(CHUNKS + 1):
        if c < CHUNKS:
            tiles += [("e1", c, i) for i in range(HALVES * EX)]
            tiles += [("gt", c)]
        if c:
            for i in range(4):
                tiles += [("e2", c - 1, i), ("g", c - 1, i)]
            tiles.append(("fin", c - 1))
    return {t: (i % BANKS, i // BANKS) for i, t in enumerate(tiles)}


def audio_tower_kernel(nc, xblk, wpack, out):
    plan = psum_plan()
    each = range(CHUNKS)
    with ExitStack() as ctx:
        def sb(name, *free):
            return ctx.enter_context(nc.sbuf_tensor(name, [P, *free], F32))

        def sem(name):
            return ctx.enter_context(nc.semaphore(name))

        bank = [ctx.enter_context(nc.psum_tensor(f"bank{i}", [P, 512], F32)) for i in range(BANKS)]
        filled = [sem(f"filled{i}") for i in range(BANKS)]
        drained = [sem(f"drained{i}") for i in range(BANKS)]

        GT = CHUNKS * NT * HALVES
        W = sb("W", PACKW)
        X = sb("X", CHUNKS, HALVES, CB, BLOCKS)
        tokW = sb("tokW_centred", 2 * D + 1)
        eps = sb("eps", 1)
        sq = sb("sq", CHUNKS, CW)
        lnv = sb("lnv", CHUNKS, CW)
        rstd = sb("rstd", CHUNKS, CW)
        z = sb("z", CHUNKS, CW)
        h0 = sb("h0", CHUNKS, CW)
        x1 = sb("x1", CHUNKS, CW)
        q = sb("q", CHUNKS, PADW)
        k = sb("k", CHUNKS, CW)
        v = sb("v", CHUNKS, CB, P)
        mx = sb("mx", CHUNKS, CB)
        e = sb("e", CHUNKS, CW)
        rsum = sb("rsum", CHUNKS, CB)
        rinv = sb("rinv", CHUNKS, CB)
        pT = sb("pT", CHUNKS, CB, HALVES, TOK)
        at = sb("at", CHUNKS, CW)
        hl = sb("hl", CHUNKS, CW)
        stats = sb("stats", CHUNKS, 6)
        bn = sb("bn", 12)
        h01 = sb("h01", CHUNKS, CW)
        h1 = sb("h1", CHUNKS, CW)
        x2 = sb("x2", CHUNKS, CW)
        lg = sb("lg", NT * HALVES, NE)
        lmx = sb("lmx", NT * HALVES)
        first = sb("first", NT * HALVES, NE)
        onehot = sb("onehot", 2, NT, P)
        ohT = sb("ohT", CHUNKS, CW)
        hid = sb("hid", 2, HALVES * MT, CW)
        h2 = sb("h2", CHUNKS, CW)
        x3 = sb("x3", CHUNKS, PADW)
        kf = sb("kf", CHUNKS, PADW)
        gl = sb("gl", GT, EX)
        ga = sb("ga", GT, EX)
        gc = sb("gc", GT, EX)
        gm1 = sb("gm1", GT, EX)
        gm2 = sb("gm2", GT, EX)
        gs = sb("gs", 8, GT)
        gp = sb("gp", CHUNKS, NT, P)
        k1, q1, qf, st = q, k, e, hl
        v3 = X[:, :, :, :, :].rearrange("p c h b t -> p (c h b t)")[:, 0:CHUNKS * CB * D].rearrange(
            "p (c b d) -> p c b d", c=CHUNKS, b=CB)
        h3, x4, s1, s2, gT, res = h1, x1, z, (h0, h01), x2, h2
        ge = pT[:, :, :, :, :].rearrange("p c b h t -> p (c b h t)").rearrange("p (u i n) -> p u i n", u=2, i=4)
        e2 = v[:, :, :, :].rearrange("p c b d -> p (c b d)")[:, 0:8 * CW].rearrange("p (u i n) -> p u i n", u=2, i=4)

        def w(name, lo=0, n=None, rows=slice(0, P)):
            n = WIDTH[name] if n is None else n
            return W[rows, COL[name] + lo:COL[name] + lo + n]

        x_loaded = [sem(f"x_loaded{c}") for c in each]
        w_loaded = [sem(f"w_loaded{i}") for i in range(3)]
        out_stored = sem("out_stored")
        constants = sem("constants")
        sq_ready = [sem(f"sq_ready{i}") for i in range(5)]
        ln_ready = [sem(f"ln_ready{i}") for i in range(5)]
        rstd_ready = [sem(f"rstd_ready{i}") for i in range(5)]
        h0_ready, h01_ready, h1_ready = sem("h0_ready"), sem("h01_ready"), sem("h1_ready")
        max_ready, e_ready, sum_ready = sem("max_ready"), sem("e_ready"), sem("sum_ready")
        inv_ready, p_ready = sem("inv_ready"), sem("p_ready")
        stats_ready, bn_step, bn_ln, bn_rstd, y_ready = (sem(n) for n in ("stats_ready", "bn_step", "bn_ln", "bn_rstd", "y_ready"))
        route_step, oh_ready = sem("route_step"), sem("oh_ready")
        k_folded, q_folded, kf_ready, qf_ready = (sem(n) for n in ("k_folded", "q_folded", "kf_ready", "qf_ready"))
        gate_step, gate_exp, gp_ready = sem("gate_step"), sem("gate_exp"), sem("gp_ready")

        def ps(tile, rows=slice(0, P), n=CW):
            return bank[plan[tile][0]][rows, 0:n]

        def claim(pe, tile):
            b, use = plan[tile]
            if use:
                pe.wait_ge(drained[b], use)

        def full(tile):
            return filled[plan[tile][0]]

        def arrived(eng, tile):
            b, use = plan[tile]
            eng.wait_ge(filled[b], use + 1)

        def free(tile):
            return drained[plan[tile][0]]

        def evacuated(eng, tile):
            b, use = plan[tile]
            eng.wait_ge(drained[b], use + 1)

        half = [slice(D * h, D * h + D) for h in range(HALVES)]
        block = ctx.enter_context(nc.Block())

        @block.sync
        def _(sp):
            sp.dma_start(W[:, 0:CUT1], wpack[:, 0:CUT1]).then_inc(w_loaded[0], 16)
            for c in each:
                sp.dma_start(X[:, c], xblk[:, c]).then_inc(x_loaded[c], 16)
            sp.dma_start(W[:, CUT1:CUT2], wpack[:, CUT1:CUT2]).then_inc(w_loaded[1], 16)
            sp.dma_start(W[:, CUT2:PACKW], wpack[:, CUT2:PACKW]).then_inc(w_loaded[2], 16)
            for c in each:
                evacuated(sp, ("fin", c))
                sp.dma_start(out[:, c], res[:, c, :]).then_inc(out_stored, 16)
            sp.wait_ge(out_stored, 16 * CHUNKS)

        @block.tensor
        def _(pe):
            mm = nc.tensor.matmul

            def centre(i, src, c):
                t = (f"cen{i}", c)
                claim(pe, t)
                mm(ps(t), w("center"), src[:, c, 0:CW], start=True, stop=True).then_inc(full(t), 1)

            def variance(i, c):
                pe.wait_ge(sq_ready[i], c + 1)
                t = (f"var{i}", c)
                claim(pe, t)
                mm(ps(t), w("mean"), sq[:, c, :], start=True, stop=True).then_inc(full(t), 1)

            pe.wait_ge(w_loaded[0], 16)
            for i in range(2):
                mm(bank[0][:, i * D:i * D + D], w("tokW", i * P, P, half[0]), w("center", 0, D, half[0]),
                   start=True, stop=True)
            mm(bank[0][:, 2 * D:2 * D + 1], w("center"), w("tokb"), start=True, stop=True).then_inc(full("setup"), 1)
            evacuated(pe, "setup")
            for c in each:
                pe.wait_ge(x_loaded[c], 16)
                claim(pe, ("tok", c))
                for i in range(2):
                    for h in range(HALVES):
                        last = mm(ps(("tok", c), half[h]), tokW[:, i * D:i * D + D], X[:, c, h, :, i:i + TOK],
                                  start=(i == 0), stop=(i == 1))
                last.then_inc(full(("tok", c)), 1)
            for c in each:
                variance(0, c)
            for c in each:
                pe.wait_ge(h0_ready, c + 1)
                centre(1, h0, c)
            for c in each:
                variance(1, c)
            pe.wait_ge(w_loaded[1], 16)
            for c in each:
                evacuated(pe, ("cen1", c))
                for n, wn in (("q", "Wq"), ("k", "Wk")):
                    claim(pe, (n, c))
                    mm(ps((n, c)), w(wn), x1[:, c, :], start=True, stop=True).then_inc(full((n, c)), 1)
            for c in each:
                for j, n in enumerate(("va", "vb")):
                    claim(pe, (n, c))
                    for i in range(CB // 2):
                        b = j * (CB // 2) + i
                        last = mm(bank[plan[(n, c)][0]][0:TOK, i * P:i * P + P], x1[:, c, b * TOK:b * TOK + TOK],
                                  w("Wv"), start=True, stop=True)
                    last.then_inc(full((n, c)), 1)
            pe.wait_ge(constants, 6)
            for c in each:
                evacuated(pe, ("q", c))
                evacuated(pe, ("k", c))
                claim(pe, ("s", c))
                for b in range(CB):
                    for h in range(HALVES):
                        last = mm(bank[plan[("s", c)][0]][half[h], b * TOK:b * TOK + TOK],
                                  q[half[h], c, b * TOK:b * TOK + D], k[half[h], c, b * TOK:b * TOK + TOK],
                                  start=True, stop=True)
                last.then_inc(full(("s", c)), 1)
            for c in each:
                pe.wait_ge(p_ready, c + 1)
                for j, n in enumerate(("pta", "ptb")):
                    claim(pe, (n, c))
                    for i in range(CB // 2):
                        b = j * (CB // 2) + i
                        last = nc.tensor.transpose(bank[plan[(n, c)][0]][0:TOK, i * P:i * P + P],
                                                   e[:, c, b * TOK:b * TOK + TOK], w("ident"))
                    last.then_inc(full((n, c)), 1)
            for c in each:
                for n in ("va", "vb", "pta", "ptb"):
                    evacuated(pe, (n, c))
                claim(pe, ("pv", c))
                for b in range(CB):
                    for h in range(HALVES):
                        last = mm(bank[plan[("pv", c)][0]][half[h], b * TOK:b * TOK + TOK],
                                  v[0:TOK, c, b, half[h]], pT[0:TOK, c, b, h, :], start=True, stop=True)
                last.then_inc(full(("pv", c)), 1)
            for c in each:
                evacuated(pe, ("pv", c))
                claim(pe, ("wl", c))
                mm(ps(("wl", c)), w("Wl"), at[:, c, :], start=True, stop=True).then_inc(full(("wl", c)), 1)
            pe.wait_ge(bn_step, 1)
            claim(pe, "bn1")
            mm(ps("bn1", n=2), w("avg"), bn[:, 0:2], start=True, stop=True).then_inc(full("bn1"), 1)
            pe.wait_ge(bn_step, 3)
            claim(pe, "bn2")
            mm(ps("bn2", n=1), w("avg"), bn[:, 5:6], start=True, stop=True).then_inc(full("bn2"), 1)
            for c in each:
                pe.wait_ge(h1_ready, c + 1)
                centre(2, h1, c)
            for c in each:
                variance(2, c)
            pe.wait_ge(w_loaded[2], 16)
            for c in each:
                evacuated(pe, ("cen2", c))
                claim(pe, ("lg", c))
                for t in range(NT):
                    last = mm(bank[plan[("lg", c)][0]][0:TT, t * HALVES * NE:(t + 1) * HALVES * NE],
                              x2[:, c, t * TT:t * TT + TT], w("router"), start=True, stop=True)
                last.then_inc(full(("lg", c)), 1)
            for c in each:
                pe.wait_ge(oh_ready, c + 1)
                claim(pe, ("oh", c))
                for t in range(NT):
                    last = nc.tensor.transpose(bank[plan[("oh", c)][0]][:, t * TT:t * TT + TT],
                                               onehot[0:TT, c % 2, t, :], w("ident", 0, TT, slice(0, TT)))
                last.then_inc(full(("oh", c)), 1)
            for c in range(CHUNKS + 1):
                if c < CHUNKS:
                    evacuated(pe, ("oh", c))
                    for i in range(HALVES * MT):
                        t = ("hid", c, i)
                        claim(pe, t)
                        mm(ps(t), w("W1", i * P, P), x2[:, c, :], start=True, stop=False)
                        mm(ps(t), w("M1", i * P, P), ohT[:, c, :], start=False, stop=True).then_inc(full(t), 1)
                if c:
                    t = ("moe", c - 1)
                    claim(pe, t)
                    for m in range(MT):
                        for h in range(HALVES):
                            evacuated(pe, ("hid", c - 1, h * MT + m))
                            mm(ps(t, half[h]), w("W2", m * D, D), hid[:, (c - 1) % 2, h * MT + m, :],
                               start=(m == 0), stop=False)
                    for h in range(HALVES):
                        last = mm(ps(t, half[h]), w("B2", h * D, D), ohT[:, c - 1, :], start=False, stop=True)
                    last.then_inc(full(t), 1)
            for c in each:
                evacuated(pe, ("moe", c))
                centre(3, h2, c)
            for c in each:
                variance(3, c)
            for c in each:
                evacuated(pe, ("cen3", c))
                for n in ("k1", "q1"):
                    claim(pe, (n, c))
                    mm(ps((n, c)), w(n[0] + "w1"), x3[:, c, 0:CW], start=True, stop=True).then_inc(full((n, c)), 1)
            for c in each:
                claim(pe, ("v3", c))
                for b in range(CB):
                    for h in range(HALVES):
                        last = mm(bank[plan[("v3", c)][0]][half[h], b * D:b * D + D],
                                  x3[half[h], c, b * TOK:b * TOK + D], w("vw", 0, D, half[h]), start=True, stop=True)
                last.then_inc(full(("v3", c)), 1)
            for c in each:
                for n, first_layer, src in (("k2", "k1", k1), ("q2", "q1", q1)):
                    evacuated(pe, (first_layer, c))
                    claim(pe, (n, c))
                    mm(ps((n, c)), w(n[0] + "w2"), src[:, c, 0:CW], start=True, stop=True).then_inc(full((n, c)), 1)
            for c in each:
                pe.wait_ge(kf_ready, c + 1)
                pe.wait_ge(qf_ready, c + 1)
                claim(pe, ("st", c))
                for b in range(CB):
                    for h in range(HALVES):
                        last = mm(bank[plan[("st", c)][0]][half[h], b * TOK:b * TOK + TOK],
                                  kf[half[h], c, b * TOK:b * TOK + D], qf[half[h], c, b * TOK:b * TOK + TOK],
                                  start=True, stop=True)
                last.then_inc(full(("st", c)), 1)
            for c in each:
                evacuated(pe, ("v3", c))
                evacuated(pe, ("st", c))
                claim(pe, ("ret", c))
                for b in range(CB):
                    for h in range(HALVES):
                        rows = slice(D * h, D * h + TOK)
                        last = mm(bank[plan[("ret", c)][0]][half[h], b * TOK:b * TOK + TOK],
                                  v3[rows, c, b, :], st[rows, c, b * TOK:b * TOK + TOK], start=True, stop=True)
                last.then_inc(full(("ret", c)), 1)
            for c in each:
                evacuated(pe, ("ret", c))
                centre(4, h3, c)
            for c in each:
                variance(4, c)
            claim(pe, "gate")
            for c in each:
                evacuated(pe, ("cen4", c))
                for t in range(NT):
                    at0 = (c * NT + t) * HALVES * EX
                    last = mm(bank[plan["gate"][0]][0:TT, at0:at0 + HALVES * EX], x4[:, c, t * TT:t * TT + TT],
                              w("gW"), start=True, stop=True)
            last.then_inc(full("gate"), 1)
            for c in each:
                claim(pe, ("s1", c))
                mm(ps(("s1", c)), w("sW1"), x4[:, c, :], start=True, stop=True).then_inc(full(("s1", c)), 1)
            for c in each:
                evacuated(pe, ("s1", c))
                for h, n in enumerate(("s2a", "s2b")):
                    claim(pe, (n, c))
                    mm(ps((n, c)), w("sW2", h * P, P), s1[:, c, :], start=True, stop=True).then_inc(full((n, c)), 1)
            for c in range(CHUNKS + 1):
                if c < CHUNKS:
                    for i in range(HALVES * EX):
                        t = ("e1", c, i)
                        claim(pe, t)
                        mm(ps(t), w("eW1", i * P, P), x4[:, c, :], start=True, stop=True).then_inc(full(t), 1)
                    pe.wait_ge(gp_ready, 1)
                    t = ("gt", c)
                    claim(pe, t)
                    for n in range(NT):
                        last = nc.tensor.transpose(bank[plan[t][0]][:, n * TT:n * TT + TT], gp[0:TT, c, n, :],
                                                   w("ident", 0, TT, slice(0, TT)))
                    last.then_inc(full(t), 1)
                if c:
                    evacuated(pe, ("gt", c - 1))
                    for i in range(4):
                        h, pair = i // 2, i % 2
                        t = ("e2", c - 1, i)
                        claim(pe, t)
                        for j in range(2):
                            x = 2 * pair + j
                            evacuated(pe, ("e1", c - 1, h * EX + x))
                            last = mm(ps(t, half[j]), w("eW2", x * D, D), hid[:, (c - 1) % 2, h * EX + x, :],
                                      start=True, stop=True)
                        last.then_inc(full(t), 1)
                        t = ("g", c - 1, i)
                        claim(pe, t)
                        mm(ps(t), w("gsel", i * P, P), gT[:, c - 1, :], start=True, stop=True).then_inc(full(t), 1)
                    t = ("fin", c - 1)
                    claim(pe, t)
                    for h, n in enumerate(("s2a", "s2b")):
                        evacuated(pe, (n, c - 1))
                        mm(ps(t, half[h]), w("sW3"), s2[h][:, c - 1, :], start=True, stop=False)
                    for h in range(HALVES):
                        mm(ps(t, half[h]), w("eB3", h * D, D), gT[:, c - 1, :], start=False, stop=False)
                    for pair in range(2):
                        for h in range(HALVES):
                            evacuated(pe, ("g", c - 1, 2 * h + pair))
                            last = mm(ps(t, half[h]), w("eW3", pair * D, D), ge[:, (c - 1) % 2, 2 * h + pair, :],
                                      start=False, stop=(pair == 1))
                    last.then_inc(full(t), 1)

        @block.scalar
        def _(act):
            f = nc.scalar.activation

            def norm(i, tile, bias=0.0):
                for c in each:
                    arrived(act, (tile, c))
                    f(sq[:, c, :], ps((tile, c)), ACT.Square, bias=bias).then_inc(sq_ready[i], 1)
                for c in each:
                    t = (f"var{i}", c)
                    arrived(act, t)
                    f(lnv[:, c, :], ps(t), ACT.Ln, bias=eps[:, 0:1]).then_inc(free(t), 1)
                for c in each:
                    evacuated(act, (f"var{i}", c))
                    f(rstd[:, c, :], lnv[:, c, :], ACT.Exp, scale=-0.5).then_inc(rstd_ready[i], 1)

            act.wait_ge(constants, 6)
            evacuated(act, "setup")
            norm(0, "tok", tokW[:, 2 * D:2 * D + 1])
            for c in each:
                evacuated(act, ("tok", c))
                f(h0[:, c, :], z[:, c, :], ACT.Identity, bias=w("tokbeta"), scale=w("tokg")).then_inc(h0_ready, 1)
            norm(1, "cen1")
            act.wait_ge(w_loaded[1], 16)
            for c in each:
                arrived(act, ("q", c))
                f(q[:, c, 0:CW], ps(("q", c)), ACT.Identity, bias=w("bq")).then_inc(free(("q", c)), 1)
            for c in each:
                arrived(act, ("va", c))
                f(v[0:TOK, c, 0:CB // 2, :], bank[plan[("va", c)][0]][0:TOK, :].rearrange("p (b d) -> p b d", d=P),
                  ACT.Copy).then_inc(free(("va", c)), 1)
            for c in each:
                evacuated(act, ("s", c))
                f(e[:, c, :], e[:, c, :], ACT.Exp, scale=1.0 / D).then_inc(e_ready, 1)
            for c in each:
                arrived(act, ("pta", c))
                f(pT[0:TOK, c, 0:CB // 2, :, :],
                  bank[plan[("pta", c)][0]][0:TOK, :].rearrange("p (b h n) -> p b h n", h=HALVES, n=D)[:, :, :, 0:TOK],
                  ACT.Copy).then_inc(free(("pta", c)), 1)
            for c in each:
                arrived(act, ("wl", c))
                f(hl[:, c, :], ps(("wl", c)), ACT.Identity, bias=w("bl")).then_inc(free(("wl", c)), 1)
            evacuated(act, "bn2")
            f(bn[:, 7:8], bn[:, 6:7], ACT.Ln, bias=eps[:, 0:1]).then_inc(bn_ln, 1)
            act.wait_ge(bn_ln, 1)
            f(bn[:, 8:9], bn[:, 7:8], ACT.Exp, scale=-0.5).then_inc(bn_rstd, 1)
            act.wait_ge(bn_step, 6)
            act.wait_ge(stats_ready, CHUNKS)
            for c in each:
                f(hl[:, c, :], hl[:, c, :], ACT.Relu, bias=bn[:, 11:12], scale=bn[:, 9:10]).then_inc(y_ready, 1)
            norm(2, "cen2")
            act.wait_ge(w_loaded[2], 16)
            for c in each:
                if c >= 2:
                    arrived(act, ("moe", c - 2))
                for i in range(0, HALVES * MT, 2):
                    t = ("hid", c, i)
                    arrived(act, t)
                    f(hid[:, c % 2, i, :], ps(t), ACT.Relu).then_inc(free(t), 1)
            norm(3, "cen3")
            for c in each:
                for n, dst in (("k1", k1), ("q1", q1)):
                    arrived(act, (n, c))
                    f(dst[:, c, 0:CW], ps((n, c)), ACT.Tanh, bias=w(n[0] + "b1")).then_inc(free((n, c)), 1)
            for c in each:
                for n, dst in (("k2", kf), ("q2", qf)):
                    arrived(act, (n, c))
                    f(dst[:, c, 0:CW], ps((n, c)), ACT.Tanh, bias=w(n[0] + "b2")).then_inc(free((n, c)), 1)
            for c in each:
                for folded, dst, ready in ((k_folded, kf, kf_ready), (q_folded, qf, qf_ready)):
                    act.wait_ge(folded, c + 1)
                    f(dst[:, c, 0:CW], dst[:, c, 0:CW], ACT.Sin, bias=w("sbias"), scale=w("sscale")).then_inc(ready, 1)
            norm(4, "cen4")
            act.wait_ge(gate_step, 2)
            f(ga[0:TT], gl[0:TT], ACT.Exp).then_inc(gate_exp, 1)
            act.wait_ge(gate_step, 17)
            f(gs[0:TT, 5, :], gs[0:TT, 4, :], ACT.Exp).then_inc(gate_exp, 1)
            for c in each:
                arrived(act, ("s1", c))
                f(s1[:, c, :], ps(("s1", c)), ACT.Relu, bias=w("sb1")).then_inc(free(("s1", c)), 1)
            for c in each:
                arrived(act, ("s2a", c))
                f(s2[0][:, c, :], ps(("s2a", c)), ACT.Relu, bias=w("sb2")).then_inc(free(("s2a", c)), 1)
            for c in range(CHUNKS + 1):
                if c < CHUNKS:
                    if c >= 2:
                        arrived(act, ("e2", c - 2, 3))
                    for i in range(0, HALVES * EX, 2):
                        t = ("e1", c, i)
                        arrived(act, t)
                        f(hid[:, c % 2, i, :], ps(t), ACT.Relu, bias=w("eb1", i % EX, 1)).then_inc(free(t), 1)
                if c:
                    for i in range(4):
                        t = ("e2", c - 1, i)
                        arrived(act, t)
                        if c >= 3:
                            evacuated(act, ("g", c - 3, i))
                        f(e2[:, (c - 1) % 2, i, :], ps(t), ACT.Relu, bias=w("eb2", i % 2, 1)).then_inc(free(t), 1)

        @block.gpsimd
        def _(pool):
            pool.memset(eps[:, :], EPS).then_inc(constants, 1)
            for t in (q, x3, kf):
                pool.memset(t[:, :, CW:PADW], 0.0).then_inc(constants, 1)
            pool.memset(onehot[:, :, :, :], 0.0).then_inc(constants, 1)
            pool.memset(gp[:, :, :, :], 0.0).then_inc(constants, 1)
            for c in each:
                pool.wait_ge(h0_ready, c + 1)
                evacuated(pool, ("cen1", c))
                pool.tensor_tensor(h01[:, c, :], h0[:, c, :], x1[:, c, :], ALU.add).then_inc(h01_ready, 1)

        @block.vector
        def _(dve):
            tt, ts, stt = nc.vector.tensor_tensor, nc.vector.tensor_scalar, nc.vector.scalar_tensor_tensor

            def across(column, n):
                return column.rearrange("p (g o) -> p g o", o=1).broadcast_to([column.shape[0], column.shape[1], n])

            def normalise(i, dst):
                for c in each:
                    dve.wait_ge(rstd_ready[i], c + 1)
                    t = (f"cen{i}", c)
                    tt(dst[:, c, 0:CW], ps(t), rstd[:, c, :], ALU.mult).then_inc(free(t), 1)

            arrived(dve, "setup")
            nc.vector.tensor_copy(tokW[:, :], bank[0][:, 0:2 * D + 1]).then_inc(free("setup"), 1)
            evacuated(dve, "setup")
            for c in each:
                dve.wait_ge(rstd_ready[0], c + 1)
                t = ("tok", c)
                stt(out=z[:, c, :], in0=ps(t), scalar=tokW[:, 2 * D:2 * D + 1], in1=rstd[:, c, :],
                    op0=ALU.add, op1=ALU.mult).then_inc(free(t), 1)
            normalise(1, x1)
            dve.wait_ge(w_loaded[1], 16)
            for c in each:
                arrived(dve, ("k", c))
                ts(k[:, c, :], ps(("k", c)), w("bk"), None, ALU.add).then_inc(free(("k", c)), 1)
            for c in each:
                arrived(dve, ("vb", c))
                nc.vector.tensor_copy(v[0:TOK, c, CB // 2:CB, :],
                                      bank[plan[("vb", c)][0]][0:TOK, :].rearrange("p (b d) -> p b d", d=P))\
                    .then_inc(free(("vb", c)), 1)
            for c in each:
                arrived(dve, ("s", c))
                scores = ps(("s", c)).rearrange("p (b m) -> p b m", b=CB)
                nc.vector.reduce_max(mx[:, c, :], scores, AX.X).then_inc(max_ready, 1)
                dve.wait_ge(max_ready, c + 1)
                tt(e[:, c, :].rearrange("p (b m) -> p b m", b=CB), scores, across(mx[:, c, :], TOK), ALU.subtract)\
                    .then_inc(free(("s", c)), 1)
            for c in each:
                ec = e[:, c, :].rearrange("p (b m) -> p b m", b=CB)
                dve.wait_ge(e_ready, c + 1)
                nc.vector.reduce_sum(rsum[:, c, :], ec, AX.X).then_inc(sum_ready, 1)
                dve.wait_ge(sum_ready, c + 1)
                nc.vector.reciprocal(rinv[:, c, :], rsum[:, c, :]).then_inc(inv_ready, 1)
                dve.wait_ge(inv_ready, c + 1)
                tt(ec, ec, across(rinv[:, c, :], TOK), ALU.mult).then_inc(p_ready, 1)
            for c in each:
                arrived(dve, ("ptb", c))
                nc.vector.tensor_copy(
                    pT[0:TOK, c, CB // 2:CB, :, :],
                    bank[plan[("ptb", c)][0]][0:TOK, :].rearrange("p (b h n) -> p b h n", h=HALVES, n=D)[:, :, :, 0:TOK])\
                    .then_inc(free(("ptb", c)), 1)
            for c in each:
                arrived(dve, ("pv", c))
                ts(at[:, c, :], ps(("pv", c)), w("bv"), None, ALU.add).then_inc(free(("pv", c)), 1)
            for c in each:
                evacuated(dve, ("wl", c))
                nc.vector.bn_stats(stats[:, c, :], hl[:, c, :]).then_inc(stats_ready, 1)
            dve.wait_ge(stats_ready, CHUNKS)
            nc.vector.bn_aggr(bn[:, 0:2], stats[:, :, :]).then_inc(bn_step, 1)
            arrived(dve, "bn1")
            nc.vector.tensor_copy(bn[:, 2:4], ps("bn1", n=2)).then_inc(free("bn1"), 1)
            evacuated(dve, "bn1")
            tt(bn[:, 4:5], bn[:, 0:1], bn[:, 2:3], ALU.subtract).then_inc(bn_step, 1)
            dve.wait_ge(bn_step, 2)
            tt(bn[:, 5:6], bn[:, 4:5], bn[:, 4:5], ALU.mult).then_inc(bn_step, 1)
            arrived(dve, "bn2")
            tt(bn[:, 6:7], ps("bn2", n=1), bn[:, 3:4], ALU.add).then_inc(free("bn2"), 1)
            dve.wait_ge(bn_rstd, 1)
            tt(bn[:, 9:10], bn[:, 8:9], w("bng"), ALU.mult).then_inc(bn_step, 1)
            dve.wait_ge(bn_step, 4)
            tt(bn[:, 10:11], bn[:, 2:3], bn[:, 9:10], ALU.mult).then_inc(bn_step, 1)
            dve.wait_ge(bn_step, 5)
            tt(bn[:, 11:12], w("bnb"), bn[:, 10:11], ALU.subtract).then_inc(bn_step, 1)
            for c in each:
                dve.wait_ge(y_ready, c + 1)
                dve.wait_ge(h01_ready, c + 1)
                tt(h1[:, c, :], h01[:, c, :], hl[:, c, :], ALU.add).then_inc(h1_ready, 1)
            normalise(2, x2)
            dve.wait_ge(w_loaded[2], 16)
            for c in each:
                t = ("lg", c)
                n = c * 4
                arrived(dve, t)
                tt(lg[0:TT].rearrange("p (t h) e -> p t (h e)", t=NT),
                   ps(t, slice(0, TT), NT * HALVES * NE).rearrange("p (t g) -> p t g", t=NT),
                   w("routerb", rows=slice(0, TT)).rearrange("p (o g) -> p o g", o=1).broadcast_to([TT, NT, HALVES * NE]),
                   ALU.add).then_inc(free(t), 1)
                evacuated(dve, t)
                nc.vector.reduce_max(lmx[0:TT], lg[0:TT], AX.X).then_inc(route_step, 1)
                dve.wait_ge(route_step, n + 1)
                tt(first[0:TT], lg[0:TT], across(lmx[0:TT], NE), ALU.is_equal).then_inc(route_step, 1)
                dve.wait_ge(route_step, n + 2)
                tt(first[0:TT].rearrange("p (t h) e -> p t (h e)", t=NT),
                   first[0:TT].rearrange("p (t h) e -> p t (h e)", t=NT),
                   w("rank", rows=slice(0, TT)).rearrange("p (o g) -> p o g", o=1).broadcast_to([TT, NT, HALVES * NE]),
                   ALU.mult).then_inc(route_step, 1)
                dve.wait_ge(route_step, n + 3)
                nc.vector.reduce_max(lmx[0:TT], first[0:TT], AX.X).then_inc(route_step, 1)
                dve.wait_ge(route_step, n + 4)
                dve.wait_ge(constants, 6)
                if c >= 2:
                    arrived(dve, ("oh", c - 2))
                tt(onehot[0:TT, c % 2, :, 0:HALVES * NE].rearrange("p t (h e) -> p t h e", h=HALVES),
                   first[0:TT].rearrange("p (t h) e -> p t h e", t=NT),
                   lmx[0:TT].rearrange("p (t h o) -> p t h o", t=NT, o=1).broadcast_to([TT, NT, HALVES, NE]),
                   ALU.is_equal).then_inc(oh_ready, 1)
                if c:
                    t = ("oh", c - 1)
                    arrived(dve, t)
                    nc.vector.tensor_copy(ohT[:, c - 1, :], ps(t)).then_inc(free(t), 1)
            t = ("oh", CHUNKS - 1)
            arrived(dve, t)
            nc.vector.tensor_copy(ohT[:, CHUNKS - 1, :], ps(t)).then_inc(free(t), 1)
            for c in range(CHUNKS + 1):
                if c < CHUNKS:
                    if c >= 2:
                        arrived(dve, ("moe", c - 2))
                    for i in range(1, HALVES * MT, 2):
                        t = ("hid", c, i)
                        arrived(dve, t)
                        ts(hid[:, c % 2, i, :], ps(t), 0.0, None, ALU.max).then_inc(free(t), 1)
                if c:
                    t = ("moe", c - 1)
                    arrived(dve, t)
                    stt(out=h2[:, c - 1, :], in0=ps(t), scalar=0.0, in1=h1[:, c - 1, :],
                        op0=ALU.max, op1=ALU.add).then_inc(free(t), 1)
            normalise(3, x3)
            for c in each:
                t = ("v3", c)
                arrived(dve, t)
                tt(v3[:, c, :, :].rearrange("p b d -> p (b d)"), ps(t, n=CB * D), w("vb"), ALU.add).then_inc(free(t), 1)
            for c in each:
                for n, folded, dst in (("k2", k_folded, kf), ("q2", q_folded, qf)):
                    evacuated(dve, (n, c))
                    stt(out=dst[:, c, 0:CW], in0=dst[:, c, 0:CW], scalar=w("fold"), in1=dst[:, c, 0:CW],
                        op0=ALU.mult, op1=ALU.max).then_inc(folded, 1)
            for c in each:
                t = ("st", c)
                arrived(dve, t)
                tt(st[:, c, :].rearrange("p (b n) -> p b n", b=CB), ps(t).rearrange("p (b n) -> p b n", b=CB),
                   w("causal").rearrange("p (o n) -> p o n", o=1).broadcast_to([P, CB, TOK]), ALU.mult)\
                    .then_inc(free(t), 1)
            for c in each:
                t = ("ret", c)
                arrived(dve, t)
                tt(h3[:, c, :], ps(t), h2[:, c, :], ALU.add).then_inc(free(t), 1)
            normalise(4, x4)
            arrived(dve, "gate")
            G = slice(0, TT)
            tt(gl[G].rearrange("p (t h) e -> p t (h e)", h=HALVES),
               ps("gate", G, GT * EX).rearrange("p (t g) -> p t g", g=HALVES * EX),
               w("gb", rows=G).rearrange("p (o g) -> p o g", o=1).broadcast_to([TT, GT // HALVES, HALVES * EX]),
               ALU.add).then_inc(free("gate"), 1)
            evacuated(dve, "gate")
            rank = w("grank", 0, EX, G).rearrange("p (o e) -> p o e", o=1).broadcast_to([TT, GT, EX])
            nc.vector.reduce_max(gs[G, 0, :], gl[G], AX.X).then_inc(gate_step, 1)
            dve.wait_ge(gate_step, 1)
            tt(gl[G], gl[G], across(gs[G, 0, :], EX), ALU.subtract).then_inc(gate_step, 1)
            dve.wait_ge(gate_exp, 1)
            nc.vector.reduce_sum(gs[G, 1, :], ga[G], AX.X).then_inc(gate_step, 1)
            dve.wait_ge(gate_step, 3)
            nc.vector.reciprocal(gs[G, 2, :], gs[G, 1, :]).then_inc(gate_step, 1)
            dve.wait_ge(gate_step, 4)
            tt(ga[G], ga[G], across(gs[G, 2, :], EX), ALU.mult).then_inc(gate_step, 1)
            dve.wait_ge(gate_step, 5)
            nc.vector.reduce_max(gs[G, 0, :], ga[G], AX.X).then_inc(gate_step, 1)
            dve.wait_ge(gate_step, 6)
            tt(gc[G], ga[G], across(gs[G, 0, :], EX), ALU.is_equal).then_inc(gate_step, 1)
            dve.wait_ge(gate_step, 7)
            tt(gc[G], gc[G], rank, ALU.mult).then_inc(gate_step, 1)
            dve.wait_ge(gate_step, 8)
            nc.vector.reduce_max(gs[G, 3, :], gc[G], AX.X).then_inc(gate_step, 1)
            dve.wait_ge(gate_step, 9)
            tt(gm1[G], gc[G], across(gs[G, 3, :], EX), ALU.is_equal).then_inc(gate_step, 1)
            dve.wait_ge(gate_step, 10)
            stt(out=gl[G], in0=gm1[G], scalar=-2.0, in1=ga[G], op0=ALU.mult, op1=ALU.add).then_inc(gate_step, 1)
            dve.wait_ge(gate_step, 11)
            nc.vector.reduce_max(gs[G, 1, :], gl[G], AX.X).then_inc(gate_step, 1)
            dve.wait_ge(gate_step, 12)
            tt(gc[G], gl[G], across(gs[G, 1, :], EX), ALU.is_equal).then_inc(gate_step, 1)
            dve.wait_ge(gate_step, 13)
            tt(gc[G], gc[G], rank, ALU.mult).then_inc(gate_step, 1)
            dve.wait_ge(gate_step, 14)
            nc.vector.reduce_max(gs[G, 3, :], gc[G], AX.X).then_inc(gate_step, 1)
            dve.wait_ge(gate_step, 15)
            tt(gm2[G], gc[G], across(gs[G, 3, :], EX), ALU.is_equal).then_inc(gate_step, 1)
            tt(gs[G, 4, :], gs[G, 1, :], gs[G, 0, :], ALU.subtract).then_inc(gate_step, 1)
            dve.wait_ge(gate_exp, 2)
            ts(gs[G, 6, :], gs[G, 5, :], 1.0, None, ALU.add).then_inc(gate_step, 1)
            dve.wait_ge(gate_step, 18)
            nc.vector.reciprocal(gs[G, 2, :], gs[G, 6, :]).then_inc(gate_step, 1)
            dve.wait_ge(gate_step, 19)
            tt(gs[G, 7, :], gs[G, 5, :], gs[G, 2, :], ALU.mult).then_inc(gate_step, 1)
            tt(gm1[G], gm1[G], across(gs[G, 2, :], EX), ALU.mult).then_inc(gate_step, 1)
            dve.wait_ge(gate_step, 20)
            tt(gm2[G], gm2[G], across(gs[G, 7, :], EX), ALU.mult).then_inc(gate_step, 1)
            dve.wait_ge(gate_step, 22)
            tt(gp[G, :, :, 0:HALVES * EX].rearrange("p c t g -> p (c t) g"),
               gm1[G].rearrange("p (t h) e -> p t (h e)", h=HALVES),
               gm2[G].rearrange("p (t h) e -> p t (h e)", h=HALVES), ALU.add).then_inc(gp_ready, 1)
            for c in each:
                t = ("s2b", c)
                arrived(dve, t)
                ts(s2[1][:, c, :], ps(t), w("sb2"), 0.0, ALU.add, ALU.max).then_inc(free(t), 1)
            for c in range(CHUNKS + 1):
                if c < CHUNKS:
                    if c >= 2:
                        arrived(dve, ("e2", c - 2, 3))
                    for i in range(1, HALVES * EX, 2):
                        t = ("e1", c, i)
                        arrived(dve, t)
                        ts(hid[:, c % 2, i, :], ps(t), w("eb1", i % EX, 1), 0.0, ALU.add, ALU.max)\
                            .then_inc(free(t), 1)
                    t = ("gt", c)
                    arrived(dve, t)
                    nc.vector.tensor_copy(gT[:, c, :], ps(t)).then_inc(free(t), 1)
                if c:
                    for i in range(4):
                        t = ("g", c - 1, i)
                        arrived(dve, t)
                        evacuated(dve, ("e2", c - 1, i))
                        tt(ge[:, (c - 1) % 2, i, :], ps(t), e2[:, (c - 1) % 2, i, :], ALU.mult).then_inc(free(t), 1)
                    t = ("fin", c - 1)
                    arrived(dve, t)
                    stt(out=res[:, c - 1, :], in0=ps(t), scalar=w("sb3"), in1=h3[:, c - 1, :],
                        op0=ALU.add, op1=ALU.add).then_inc(free(t), 1)


def pack_weights(a):
    pack = np.zeros((P, PACKW), np.float32)

    def put(name, block, row=0, lo=0):
        pack[row:row + block.shape[0], COL[name] + lo:COL[name] + lo + block.shape[1]] = block

    def both(name, block):
        for h in range(HALVES):
            put(name, block, D * h, block.shape[1] * h)

    def column(name, vec, lo=0):
        for r in range(0, P, len(vec)):
            put(name, vec[:, None], r, lo)

    eye = np.eye(D, dtype=np.float32)
    ones = np.ones((D, D), np.float32)
    put("tokW", a["L0_tok_W"])
    both("center", eye - np.float32(1.0 / D) * ones)
    both("mean", np.float32(1.0 / D) * ones)
    column("tokb", a["L0_tok_b"])
    column("tokg", a["L0_tok_gamma"])
    column("tokbeta", a["L0_tok_beta"])
    for n in "qkvl":
        both("W" + n, a["L0_attn_W" + n])
        column("b" + n, a["L0_attn_b" + n])
    column("bng", a["L0_attn_gamma"])
    column("bnb", a["L0_attn_beta"])
    pack[:, COL["avg"]:COL["avg"] + P] = np.tile(np.float32(0.5) * eye, (2, 2))
    put("ident", np.eye(P, dtype=np.float32))
    both("router", a["L0_ffn_router_w"].T)
    put("routerb", np.tile(a["L0_ffn_router_b"], (P, HALVES)))
    put("rank", np.tile(np.arange(NE, 0, -1, dtype=np.float32), (P, HALVES)))
    w1 = a["L0_ffn_W1"].transpose(1, 0, 2).reshape(D, NE * NH)
    own = np.full((NE, NE, NH), -BIG, np.float32)
    own[np.arange(NE), np.arange(NE)] = a["L0_ffn_b1"]
    w2 = a["L0_ffn_W2"].reshape(NE * NH, D)
    for h in range(HALVES):
        put("W1", w1, D * h, h * MT * P)
        put("M1", own.reshape(NE, NE * NH), NE * h, h * MT * P)
        put("B2", a["L0_ffn_b2"], NE * h, h * D)
    for m in range(MT):
        put("W2", w2[m * P:m * P + P], 0, m * D)
    for n in "kq":
        both(n + "w1", a[f"L1_attn_{n}w1"].T)
        both(n + "w2", np.tile(a[f"L1_attn_{n}w2"].T, (1, 2)))
        column(n + "b1", a[f"L1_attn_{n}b1"])
        column(n + "b2", a[f"L1_attn_{n}b2"])
    for h in range(HALVES):
        put("vw", a["L1_attn_vw"].T, D * h)
    put("vb", np.tile(a["L1_attn_vb"], (P, CB)))
    m, n = np.arange(P)[:, None] % D, np.arange(TOK)[None]
    put("causal", np.where(m <= n, 1.0 / np.sqrt((n + 1.0) * KP), 0.0).astype(np.float32))
    cosine = (np.arange(P) % D < KP)
    column("fold", np.where(cosine, -1.0, 1.0).astype(np.float32))
    column("sscale", np.where(cosine, -np.pi, np.pi).astype(np.float32))
    column("sbias", np.where(cosine, np.pi / 2, 0.0).astype(np.float32))
    both("gW", a["L1_ffn_gW"])
    put("gb", np.tile(a["L1_ffn_gb"], (P, HALVES)))
    put("grank", np.tile(np.arange(EX, 0, -1, dtype=np.float32), (P, HALVES)))
    both("sW1", a["L1_ffn_sW1"])
    put("sW3", a["L1_ffn_sW3"])
    column("sb1", a["L1_ffn_sb1"])
    column("sb2", a["L1_ffn_sb2"])
    column("sb3", a["L1_ffn_sb3"])
    for h in range(HALVES):
        put("sW2", a["L1_ffn_sW2"], D * h, h * P)
        put("eB3", a["L1_ffn_eb3"], EX * h, h * D)
        for x in range(EX):
            put("eW1", a["L1_ffn_eW1"][x], D * h, (h * EX + x) * P)
            pair, j = x // 2, x % 2
            put("gsel", np.ones((1, D), np.float32), h * EX + x, (2 * h + pair) * P + j * D)
    for x in range(EX):
        put("eW2", a["L1_ffn_eW2"][x], 0, x * D)
        put("eW3", a["L1_ffn_eW3"][x], D * (x % 2), (x // 2) * D)
        column("eb1", a["L1_ffn_eb1"][x], x)
        put("eb2", a["L1_ffn_eb2"][x][:, None], D * (x % 2), x // 2)
    return pack


def kernel(**inputs):
    import concourse.bacc as bacc
    from concourse.bass_utils import run_bass_kernel_spmd

    a = {n: np.asarray(x) for n, x in inputs.items()}
    x = a["x"][:, :BLOCKS * STRIDE].reshape(HALVES, CHUNKS, CB, BLOCKS, STRIDE * FEAT)
    arrays = {"xblk": np.ascontiguousarray(x.transpose(4, 1, 0, 2, 3)), "wpack": pack_weights(a)}
    nc = bacc.Bacc("TRN2", target_bir_lowering=False, num_devices=1)
    args = [nc.dram_tensor(n, v.shape, F32, kind="ExternalInput").ap() for n, v in arrays.items()]
    out = nc.dram_tensor("out", (P, CHUNKS, CW), F32, kind="ExternalOutput").ap()
    audio_tower_kernel(nc, *args, out)
    r = run_bass_kernel_spmd(nc, [arrays], core_ids=[0])
    o = r.results[0]["out"].reshape(HALVES, D, CHUNKS, CB, TOK)
    return np.ascontiguousarray(o.transpose(0, 2, 3, 4, 1)).reshape(B, TOK, D)
```

```python
from contextlib import ExitStack

import numpy as np
import concourse.bass as bass
from concourse import mybir

B, SEQ, FEAT = 64, 375, 16
PATCH, STRIDE, D = 16, 8, 64
TOK = (SEQ - PATCH) // STRIDE + 1
BLOCKS = TOK + PATCH // STRIDE - 1
P = 128
HALVES = P // D
HB = B // HALVES
CHUNKS = 4
CB = HB // CHUNKS
CW = CB * TOK
PADW = CW + D - TOK
CJ = CB // 2
TT = 60
NT = CW // (2 * TT)
NE, NH = 32, 16
MT = NE * NH // P
KP = 32
SH1, SH2, EH1, EH2, EX = 64, 128, 128, 64, 4
BANKS = 8
BIG = 2.0 ** 100
EPS = 1e-5

F32 = mybir.dt.float32
F32R = mybir.dt.float32r
BF16 = mybir.dt.bfloat16
ALU = mybir.AluOpType
ACT = mybir.ActivationFunctionType
LN_EXP = "natural_log_exp_and_others"
AX = mybir.AxisListType

PACK = [
    ("tokW", PATCH * FEAT), ("center", P), ("mean", P), ("tokb", 1), ("tokg", 1), ("tokbeta", 1),
    ("Wq", P), ("Wk", P), ("Wv", P), ("Wl", P), ("bq", 1), ("bk", 1), ("bv", 1), ("bl", 1),
    ("bng", 1), ("bnb", 1), ("avg", P), ("ident", P),
    ("router", HALVES * NE), ("routerb", HALVES * NE), ("rank", HALVES * NE),
    ("W1", MT * P), ("M1", HALVES * MT * P), ("W2", MT * D), ("B2", P),
    ("kw1", P), ("qw1", P), ("kw2", P), ("qw2", P), ("vw", P), ("vb", CB * D), ("causal", TOK),
    ("kb1", 1), ("qb1", 1), ("kb2", 1), ("qb2", 1), ("fold", 1), ("sscale", 1), ("sbias", 1),
    ("gW", HALVES * EX), ("gb", HALVES * EX), ("grank", HALVES * EX),
    ("sW1", P), ("sW2", HALVES * P), ("sW3", D), ("eW1", EX * P), ("eW2", EX * D),
    ("eW3", 2 * D), ("eB3", P), ("gsel", HALVES * 2 * P),
    ("sb1", 1), ("sb2", 1), ("sb3", 1), ("eb1", EX), ("eb2", 2),
]
COL, WIDTH = {}, dict(PACK)
_at = 0
for _n, _w in PACK:
    COL[_n] = _at
    _at += _w
PACKW = _at
CUT1 = COL["Wq"]
CUT2 = COL["router"]


def psum_plan():
    tiles = ["setup"]
    each = range(CHUNKS)

    def stage(*names):
        tiles.extend((n, c) for c in each for n in names)

    stage("tok"), stage("var0")
    stage("cen1"), stage("var1")
    stage("q", "k"), stage("v")
    stage("s"), stage("pta", "ptb"), stage("pv"), stage("wl")
    tiles += ["bn1", "bn2"]
    stage("cen2"), stage("var2")
    stage("lg"), stage("oh")
    for c in range(CHUNKS + 1):
        if c < CHUNKS:
            tiles += [("hid", c, i) for i in range(HALVES * MT)]
        if c:
            tiles.append(("moe", c - 1))
    stage("cen3"), stage("var3")
    stage("k1", "q1"), stage("v3"), stage("k2", "q2")
    stage("st"), stage("ret")
    stage("cen4"), stage("var4")
    tiles.append("gate")
    stage("s1"), stage("s2a", "s2b")
    for c in range(CHUNKS + 1):
        if c < CHUNKS:
            tiles += [("e1", c, i) for i in range(HALVES * EX)]
            tiles += [("gt", c)]
        if c:
            for i in range(4):
                tiles += [("e2", c - 1, i), ("g", c - 1, i)]
            tiles.append(("fin", c - 1))
    return {t: (i % BANKS, i // BANKS) for i, t in enumerate(tiles)}


def audio_tower_kernel(nc, xblk, wpack, out):
    plan = psum_plan()
    each = range(CHUNKS)
    with ExitStack() as ctx:
        def sb(name, *free, dt=F32):
            return ctx.enter_context(nc.sbuf_tensor(name, [P, *free], dt))

        def sem(name):
            return ctx.enter_context(nc.semaphore(name))

        bank = [ctx.enter_context(nc.psum_tensor(f"bank{i}", [P, 512], F32)) for i in range(BANKS)]
        filled = [sem(f"filled{i}") for i in range(BANKS)]
        drained = [sem(f"drained{i}") for i in range(BANKS)]

        GT = CHUNKS * NT * HALVES
        W = sb("W", PACKW)
        X = sb("X", CHUNKS, HALVES, CB, BLOCKS)
        tokW = sb("tokW_centred", 2 * D + 1)
        eps = sb("eps", 1)
        sq = sb("sq", CHUNKS, CW)
        lnv = sb("lnv", 2, CW)
        rstd = sb("rstd", CHUNKS, CW)
        z = sb("z", CHUNKS, CW)
        h0 = sb("h0", CHUNKS, CW)
        x1 = sb("x1", CHUNKS, PADW)
        q = sb("q", CHUNKS, PADW)
        diag = sb("diag", CHUNKS, CB, HALVES, TOK)
        v = sb("v", CHUNKS, CJ, HALVES, D)
        mx = sb("mx", CHUNKS, CB)
        e = sb("e", CHUNKS, PADW)
        rsum = sb("rsum", CHUNKS, CB)
        rinv = sb("rinv", CHUNKS, CB)
        pT = sb("pT", CHUNKS, CB, 2, TOK)
        stats = sb("stats", CHUNKS, 6)
        bn = sb("bn", 12)
        h01 = sb("h01", CHUNKS, CW)
        x2 = sb("x2", CHUNKS, PADW)
        lg = sb("lg", NT * HALVES, NE)
        lmx = sb("lmx", NT * HALVES)
        first = sb("first", NT * HALVES, NE)
        onehot = sb("onehot", 2, NT, 2, HALVES * NE, dt=BF16)
        routeT = sb("routeT", CHUNKS, CW, dt=F32R)
        xh = sb("xh", 2, CW, dt=F32R)
        xl = sb("xl", 2, CW, dt=F32R)
        xs = sb("xs", HALVES, CHUNKS, CW, dt=F32R)
        ident_b = sb("ident_b", P, dt=BF16)
        ident_r = sb("ident_r", P, dt=F32R)
        w1s = sb("w1s", 2, MT, P, dt=F32R)
        e1s = sb("e1s", 2, EX, P, dt=F32R)
        m1s = sb("m1s", HALVES * MT, P, dt=F32R)
        b2s = sb("b2s", P, dt=F32R)
        b3s = sb("b3s", 2, P, dt=F32R)
        gsel = sb("gsel", 4, P, dt=F32R)
        hid = sb("hid", 2, HALVES * MT, CW)
        gl = sb("gl", GT, EX)
        ga = sb("ga", GT, EX)
        gc = sb("gc", GT, EX)
        gm1 = sb("gm1", GT, EX)
        gm2 = sb("gm2", GT, EX)
        gs = sb("gs", 8, GT)
        gsum = sb("gsum", GT, EX)
        gp = sb("gp", CHUNKS, NT, P, dt=F32R)
        at, hl, x3 = z, q, x2
        twice = hid[:, :, :, :].rearrange("p u i n -> p (u i n)")[:, 0:CHUNKS * CB * 2 * D].rearrange(
            "p (c g i m) -> p c g i m", c=CHUNKS, g=CB, i=2)
        k1, kf, q1, qf = x1, x1, e, e
        spent = X[:, :, :, :, :].rearrange("p c h b t -> p (c h b t)")[:, 0:2 * CHUNKS * CW]
        h1, h2 = (spent[:, i * CHUNKS * CW:(i + 1) * CHUNKS * CW].rearrange("p (c n) -> p c n", n=CW) for i in range(2))
        h3, x4, s1, s2, ohT, gT, res = h1, x1, z, (h0, h01), routeT, routeT, h2
        ge = pT[:, :, :, :, :].rearrange("p c b h t -> p (c b h t)").rearrange("p (u i n) -> p u i n", u=2, i=4)
        e2 = diag[:, :, :, :, :].rearrange("p c b h t -> p (c b h t)").rearrange("p (u i n) -> p u i n", u=2, i=4)

        def w(name, lo=0, n=None, rows=slice(0, P)):
            n = WIDTH[name] if n is None else n
            return W[rows, COL[name] + lo:COL[name] + lo + n]

        x_loaded = [sem(f"x_loaded{c}") for c in each]
        w_loaded = [sem(f"w_loaded{i}") for i in range(3)]
        out_stored = sem("out_stored")
        CONSTANTS = 9
        constants = sem("constants")
        sq_ready = [sem(f"sq_ready{i}") for i in range(5)]
        ln_ready = [sem(f"ln_ready{i}") for i in range(5)]
        rstd_ready = [sem(f"rstd_ready{i}") for i in range(5)]
        h0_ready, h01_ready, h1_ready = sem("h0_ready"), sem("h01_ready"), sem("h1_ready")
        max_ready, e_ready, sum_ready = sem("max_ready"), sem("e_ready"), sem("sum_ready")
        inv_ready, p_ready = sem("inv_ready"), sem("p_ready")
        stats_ready, bn_step, bn_ln, bn_rstd, y_ready = (sem(n) for n in ("stats_ready", "bn_step", "bn_ln", "bn_rstd", "y_ready"))
        route_step, oh_ready = sem("route_step"), sem("oh_ready")
        k_folded, q_folded, kf_ready, qf_ready = (sem(n) for n in ("k_folded", "q_folded", "kf_ready", "qf_ready"))
        weights_split, SPLITS = sem("weights_split"), 13
        xh_ready, xl_ready = sem("xh_ready"), sem("xl_ready")
        split_moved = [sem(f"split_moved{i}") for i in range(2)]
        gate_step, gate_exp, gp_ready = sem("gate_step"), sem("gate_exp"), sem("gp_ready")

        def ps(tile, rows=slice(0, P), n=CW):
            return bank[plan[tile][0]][rows, 0:n]

        def claim(pe, tile):
            b, use = plan[tile]
            if use:
                pe.wait_ge(drained[b], use)

        def full(tile):
            return filled[plan[tile][0]]

        def arrived(eng, tile):
            b, use = plan[tile]
            eng.wait_ge(filled[b], use + 1)

        def free(tile):
            return drained[plan[tile][0]]

        def evacuated(eng, tile):
            b, use = plan[tile]
            eng.wait_ge(drained[b], use + 1)

        half = [slice(D * h, D * h + D) for h in range(HALVES)]
        block = ctx.enter_context(nc.Block())

        @block.sync
        def _(sp):
            sp.dma_start(W[:, 0:CUT1], wpack[:, 0:CUT1]).then_inc(w_loaded[0], 16)
            for c in each:
                sp.dma_start(X[:, c], xblk[:, c]).then_inc(x_loaded[c], 16)
            sp.dma_start(W[:, CUT1:CUT2], wpack[:, CUT1:CUT2]).then_inc(w_loaded[1], 16)
            sp.dma_start(W[:, CUT2:PACKW], wpack[:, CUT2:PACKW]).then_inc(w_loaded[2], 16)
            for r in range(2):
                for c in each:
                    n = CHUNKS * r + c
                    if r:
                        arrived(sp, ("hid", c, HALVES * MT - 1))
                    sp.wait_ge(xh_ready, n + 1)
                    sp.wait_ge(xl_ready, n + 1)
                    for h in range(HALVES):
                        sp.dma_start(xs[half[0], h, c, :].bitcast(F32), xh[half[h], c % 2, :].bitcast(F32)).then_inc(split_moved[n % 2], 16)
                        sp.dma_start(xs[half[1], h, c, :].bitcast(F32),
                                     xl[half[h], c % 2, :].bitcast(F32)).then_inc(split_moved[n % 2], 16)
            for c in each:
                evacuated(sp, ("fin", c))
                sp.dma_start(out[:, c], res[:, c, :]).then_inc(out_stored, 16)
            sp.wait_ge(out_stored, 16 * CHUNKS)

        @block.tensor
        def _(pe):
            mm = nc.tensor.matmul

            def centre(i, src, c):
                t = (f"cen{i}", c)
                claim(pe, t)
                mm(ps(t), w("center"), src[:, c, 0:CW], start=True, stop=True).then_inc(full(t), 1)

            def variance(i, c):
                pe.wait_ge(sq_ready[i], c + 1)
                t = (f"var{i}", c)
                claim(pe, t)
                mm(ps(t), w("mean"), sq[:, c, :], start=True, stop=True).then_inc(full(t), 1)

            def values(t, x, weight):
                claim(pe, t)
                c = t[1]
                for b in range(CB):
                    j, s = b // 2, b % 2
                    last = mm(bank[plan[t][0]][half[s], j * P:j * P + P], x[:, c, b * TOK:b * TOK + D],
                              w(weight), start=True, stop=True)
                last.then_inc(full(t), 1)

            def products(t, stationary, diagonal):
                claim(pe, t)
                c = t[1]
                for b in range(CB):
                    j, s = b // 2, b % 2
                    last = mm(bank[plan[t][0]][half[s], 2 * j * TOK:2 * (j + 1) * TOK],
                              stationary[:, c, b * TOK:b * TOK + D], diagonal[:, c, b, :, :], start=True, stop=True)
                last.then_inc(full(t), 1)

            def weighted_values(t, pairs):
                claim(pe, t)
                c = t[1]
                for j in range(CJ):
                    for h in range(HALVES):
                        last = mm(bank[plan[t][0]][half[h], 2 * j * TOK:2 * (j + 1) * TOK],
                                  v[:, c, j, h, :], pairs[:, c, HALVES * j + h, :, :], start=True, stop=True)
                last.then_inc(full(t), 1)

            pe.wait_ge(w_loaded[0], 16)
            for i in range(2):
                mm(bank[0][:, i * D:i * D + D], w("tokW", i * P, P, half[0]), w("center", 0, D, half[0]),
                   start=True, stop=True)
            mm(bank[0][:, 2 * D:2 * D + 1], w("center"), w("tokb"), start=True, stop=True).then_inc(full("setup"), 1)
            evacuated(pe, "setup")
            for c in each:
                pe.wait_ge(x_loaded[c], 16)
                claim(pe, ("tok", c))
                for i in range(2):
                    for h in range(HALVES):
                        last = mm(ps(("tok", c), half[h]), tokW[:, i * D:i * D + D], X[:, c, h, :, i:i + TOK],
                                  start=(i == 0), stop=(i == 1))
                last.then_inc(full(("tok", c)), 1)
            for c in each:
                variance(0, c)
            for c in each:
                pe.wait_ge(h0_ready, c + 1)
                centre(1, h0, c)
            for c in each:
                variance(1, c)
            pe.wait_ge(w_loaded[1], 16)
            for c in each:
                evacuated(pe, ("cen1", c))
                for n, wn in (("q", "Wq"), ("k", "Wk")):
                    claim(pe, (n, c))
                    mm(ps((n, c)), w(wn), x1[:, c, 0:CW], start=True, stop=True).then_inc(full((n, c)), 1)
            for c in each:
                values(("v", c), x1, "Wv")
            pe.wait_ge(constants, CONSTANTS)
            for c in each:
                evacuated(pe, ("q", c))
                evacuated(pe, ("k", c))
                products(("s", c), q, diag)
            for c in each:
                pe.wait_ge(p_ready, c + 1)
                for j, n in enumerate(("pta", "ptb")):
                    claim(pe, (n, c))
                    for i in range(4):
                        g = 4 * j + i
                        last = nc.tensor.transpose(bank[plan[(n, c)][0]][:, i * P:i * P + P],
                                                   twice[:, c, g].rearrange("p i m -> p (i m)"), w("ident"))
                    last.then_inc(full((n, c)), 1)
            for c in each:
                for n in ("v", "pta", "ptb"):
                    evacuated(pe, (n, c))
                weighted_values(("pv", c), pT)
            for c in each:
                evacuated(pe, ("pv", c))
                claim(pe, ("wl", c))
                mm(ps(("wl", c)), w("Wl"), at[:, c, :], start=True, stop=True).then_inc(full(("wl", c)), 1)
            pe.wait_ge(bn_step, 1)
            claim(pe, "bn1")
            mm(ps("bn1", n=2), w("avg"), bn[:, 0:2], start=True, stop=True).then_inc(full("bn1"), 1)
            pe.wait_ge(bn_step, 3)
            claim(pe, "bn2")
            mm(ps("bn2", n=1), w("avg"), bn[:, 5:6], start=True, stop=True).then_inc(full("bn2"), 1)
            for c in each:
                pe.wait_ge(h1_ready, c + 1)
                centre(2, h1, c)
            for c in each:
                variance(2, c)
            pe.wait_ge(w_loaded[2], 16)
            pe.wait_ge(weights_split, SPLITS)
            for c in each:
                evacuated(pe, ("cen2", c))
                claim(pe, ("lg", c))
                for i in range(2 * NT):
                    u, s = i // 2, i % 2
                    last = mm(bank[plan[("lg", c)][0]][half[s], u * HALVES * NE:(u + 1) * HALVES * NE],
                              x2[:, c, i * TT:i * TT + D], w("router"), start=True, stop=True)
                last.then_inc(full(("lg", c)), 1)
            for c in each:
                pe.wait_ge(oh_ready, c + 1)
                claim(pe, ("oh", c))
                for u in range(NT):
                    last = mm(bank[plan[("oh", c)][0]][:, 2 * u * TT:2 * (u + 1) * TT],
                              onehot[:, c % 2, u, :, :].rearrange("p i g -> p (i g)"),
                              ident_b[:, :].rearrange("p (s t) -> p s t", s=2)[:, :, 0:TT], start=True, stop=True)
                last.then_inc(full(("oh", c)), 1)
            for c in range(CHUNKS + 1):
                if c < CHUNKS:
                    evacuated(pe, ("oh", c))
                    pe.wait_ge(split_moved[c % 2], 64 * (c // 2 + 1))
                    for i in range(HALVES * MT):
                        h, m = i // MT, i % MT
                        t = ("hid", c, i)
                        claim(pe, t)
                        mm(ps(t), w1s[:, 0, m, :], xs[:, h, c, :], start=True, stop=False)
                        mm(ps(t), w1s[:, 1, m, :], xs[:, h, c, :], start=False, stop=False)
                        mm(ps(t), m1s[:, i, :], ohT[:, c, :], start=False, stop=True).then_inc(full(t), 1)
                if c:
                    t = ("moe", c - 1)
                    claim(pe, t)
                    mm(ps(t), b2s[:, :], ohT[:, c - 1, :], start=True, stop=False)
                    for m in range(MT):
                        for h in range(HALVES):
                            evacuated(pe, ("hid", c - 1, h * MT + m))
                            last = mm(ps(t, half[h]), w("W2", m * D, D), hid[:, (c - 1) % 2, h * MT + m, :],
                               start=False, stop=(m == MT - 1))
                    last.then_inc(full(t), 1)
            for c in each:
                evacuated(pe, ("moe", c))
                centre(3, h2, c)
            for c in each:
                variance(3, c)
            for c in each:
                evacuated(pe, ("cen3", c))
                for n in ("k1", "q1"):
                    claim(pe, (n, c))
                    mm(ps((n, c)), w(n[0] + "w1"), x3[:, c, 0:CW], start=True, stop=True).then_inc(full((n, c)), 1)
            for c in each:
                values(("v3", c), x3, "vw")
            for c in each:
                for n, first_layer, src in (("k2", "k1", k1), ("q2", "q1", q1)):
                    evacuated(pe, (first_layer, c))
                    claim(pe, (n, c))
                    mm(ps((n, c)), w(n[0] + "w2"), src[:, c, 0:CW], start=True, stop=True).then_inc(full((n, c)), 1)
            for c in each:
                pe.wait_ge(kf_ready, c + 1)
                pe.wait_ge(qf_ready, c + 1)
                products(("st", c), kf, diag)
            for c in each:
                evacuated(pe, ("v3", c))
                evacuated(pe, ("st", c))
                weighted_values(("ret", c), pT)
            for c in each:
                evacuated(pe, ("ret", c))
                centre(4, h3, c)
            for c in each:
                variance(4, c)
            claim(pe, "gate")
            for c in each:
                evacuated(pe, ("cen4", c))
                for i in range(2 * NT):
                    u, s = i // 2, i % 2
                    at0 = (c * NT + u) * HALVES * EX
                    last = mm(bank[plan["gate"][0]][half[s], at0:at0 + HALVES * EX], x4[:, c, i * TT:i * TT + D],
                              w("gW"), start=True, stop=True)
            last.then_inc(full("gate"), 1)
            for c in each:
                claim(pe, ("s1", c))
                mm(ps(("s1", c)), w("sW1"), x4[:, c, 0:CW], start=True, stop=True).then_inc(full(("s1", c)), 1)
            for c in each:
                evacuated(pe, ("s1", c))
                for h, n in enumerate(("s2a", "s2b")):
                    claim(pe, (n, c))
                    mm(ps((n, c)), w("sW2", h * P, P), s1[:, c, :], start=True, stop=True).then_inc(full((n, c)), 1)
            for c in range(CHUNKS + 1):
                if c < CHUNKS:
                    pe.wait_ge(split_moved[c % 2], 64 * ((CHUNKS + c) // 2 + 1))
                    for i in range(HALVES * EX):
                        h, x = i // EX, i % EX
                        t = ("e1", c, i)
                        claim(pe, t)
                        mm(ps(t), e1s[:, 0, x, :], xs[:, h, c, :], start=True, stop=False)
                        mm(ps(t), e1s[:, 1, x, :], xs[:, h, c, :], start=False, stop=True).then_inc(full(t), 1)
                    pe.wait_ge(gp_ready, 1)
                    t = ("gt", c)
                    claim(pe, t)
                    for u in range(NT):
                        last = mm(bank[plan[t][0]][:, 2 * u * TT:2 * (u + 1) * TT], gp[:, c, u, :],
                                  ident_r[:, :].rearrange("p (s t) -> p s t", s=2)[:, :, 0:TT], start=True, stop=True)
                    last.then_inc(full(t), 1)
                if c:
                    evacuated(pe, ("gt", c - 1))
                    for i in range(4):
                        h, pair = i // 2, i % 2
                        t = ("e2", c - 1, i)
                        claim(pe, t)
                        for j in range(2):
                            x = 2 * pair + j
                            evacuated(pe, ("e1", c - 1, h * EX + x))
                            last = mm(ps(t, half[j]), w("eW2", x * D, D), hid[:, (c - 1) % 2, h * EX + x, :],
                                      start=True, stop=True)
                        last.then_inc(full(t), 1)
                        t = ("g", c - 1, i)
                        claim(pe, t)
                        mm(ps(t), gsel[:, i, :], gT[:, c - 1, :], start=True, stop=True).then_inc(full(t), 1)
                    t = ("fin", c - 1)
                    claim(pe, t)
                    mm(ps(t), b3s[:, 0, :], gT[:, c - 1, :], start=True, stop=False)
                    mm(ps(t), b3s[:, 1, :], gT[:, c - 1, :], start=False, stop=False)
                    for h, n in enumerate(("s2a", "s2b")):
                        evacuated(pe, (n, c - 1))
                        mm(ps(t, half[h]), w("sW3"), s2[h][:, c - 1, :], start=False, stop=False)
                    for pair in range(2):
                        for h in range(HALVES):
                            evacuated(pe, ("g", c - 1, 2 * h + pair))
                            last = mm(ps(t, half[h]), w("eW3", pair * D, D), ge[:, (c - 1) % 2, 2 * h + pair, :],
                                      start=False, stop=(pair == 1))
                    last.then_inc(full(t), 1)

        @block.scalar
        def _(act):
            f = nc.scalar.activation

            def norm(i, tile, bias=0.0):
                for c in each:
                    arrived(act, (tile, c))
                    f(sq[:, c, :], ps((tile, c)), ACT.Square, bias=bias).then_inc(sq_ready[i], 1)
                for c in each:
                    t = (f"var{i}", c)
                    arrived(act, t)
                    f(lnv[:, c % 2, :], ps(t), ACT.Ln, bias=eps[:, 0:1]).then_inc(free(t), 1)
                    evacuated(act, t)
                    f(rstd[:, c, :], lnv[:, c % 2, :], ACT.Exp, scale=-0.5).then_inc(rstd_ready[i], 1)

            def split_hi(x, tile):
                for c in each:
                    evacuated(act, (tile, c))
                    n = c + (CHUNKS if tile == "cen4" else 0)
                    if n >= 2:
                        act.wait_ge(split_moved[n % 2], 64 * (n // 2))
                    f(xh[:, c % 2, :], x[:, c, 0:CW], ACT.Copy).then_inc(xh_ready, 1)

            act.preload_act_table_set(LN_EXP)
            act.wait_ge(constants, CONSTANTS)
            evacuated(act, "setup")
            norm(0, "tok", tokW[:, 2 * D:2 * D + 1])
            for c in each:
                evacuated(act, ("tok", c))
                f(h0[:, c, :], z[:, c, :], ACT.Identity, bias=w("tokbeta"), scale=w("tokg")).then_inc(h0_ready, 1)
            norm(1, "cen1")
            act.wait_ge(w_loaded[1], 16)
            for c in each:
                arrived(act, ("q", c))
                f(q[:, c, 0:CW], ps(("q", c)), ACT.Identity, bias=w("bq")).then_inc(free(("q", c)), 1)
            for c in each:
                arrived(act, ("v", c))
                f(v[:, c].rearrange("p j h d -> p (j h d)"), ps(("v", c), n=CB * D), ACT.Copy)\
                    .then_inc(free(("v", c)), 1)
            for c in each:
                evacuated(act, ("s", c))
                f(e[:, c, 0:CW], e[:, c, 0:CW], ACT.Exp, scale=1.0 / D).then_inc(e_ready, 1)
            for c in each:
                arrived(act, ("pta", c))
                for s in range(2):
                    rows = slice(D * s, D * s + TOK)
                    last = f(pT[rows, c, 0:4, s, :],
                             bank[plan[("pta", c)][0]][rows, :].rearrange("p (g s n) -> p g s n", s=2, n=D)[:, :, s, 0:TOK],
                             ACT.Copy)
                last.then_inc(free(("pta", c)), 1)
            for c in each:
                arrived(act, ("wl", c))
                f(hl[:, c, 0:CW], ps(("wl", c)), ACT.Identity, bias=w("bl")).then_inc(free(("wl", c)), 1)
            evacuated(act, "bn2")
            f(bn[:, 7:8], bn[:, 6:7], ACT.Ln, bias=eps[:, 0:1]).then_inc(bn_ln, 1)
            act.wait_ge(bn_ln, 1)
            f(bn[:, 8:9], bn[:, 7:8], ACT.Exp, scale=-0.5).then_inc(bn_rstd, 1)
            act.wait_ge(bn_step, 6)
            act.wait_ge(stats_ready, CHUNKS)
            for c in each:
                f(hl[:, c, 0:CW], hl[:, c, 0:CW], ACT.Relu, bias=bn[:, 11:12], scale=bn[:, 9:10]).then_inc(y_ready, 1)
            norm(2, "cen2")
            split_hi(x2, "cen2")
            for c in each:
                if c >= 2:
                    arrived(act, ("moe", c - 2))
                for i in range(0, HALVES * MT, 2):
                    t = ("hid", c, i)
                    arrived(act, t)
                    f(hid[:, c % 2, i, :], ps(t), ACT.Relu).then_inc(free(t), 1)
            norm(3, "cen3")
            act.preload_act_table(ACT.Tanh)
            for c in each:
                for n, dst in (("k1", k1), ("q1", q1)):
                    arrived(act, (n, c))
                    f(dst[:, c, 0:CW], ps((n, c)), ACT.Tanh, bias=w(n[0] + "b1")).then_inc(free((n, c)), 1)
            for c in each:
                for n, dst in (("k2", kf), ("q2", qf)):
                    arrived(act, (n, c))
                    f(dst[:, c, 0:CW], ps((n, c)), ACT.Tanh, bias=w(n[0] + "b2")).then_inc(free((n, c)), 1)
            act.preload_act_table(ACT.Sin)
            for c in each:
                act.wait_ge(k_folded, c + 1)
                f(kf[:, c, 0:CW], kf[:, c, 0:CW], ACT.Sin, bias=w("sbias"), scale=w("sscale")).then_inc(kf_ready, 1)
                act.wait_ge(q_folded, c + 1)
                for h in range(HALVES):
                    last = f(diag[half[h], c, :, h, :], qf[half[h], c, 0:CW].rearrange("p (b t) -> p b t", t=TOK),
                             ACT.Sin, bias=w("sbias", rows=half[h]), scale=w("sscale", rows=half[h]))
                last.then_inc(qf_ready, 1)
            act.preload_act_table_set(LN_EXP)
            norm(4, "cen4")
            split_hi(x4, "cen4")
            act.wait_ge(gate_step, 2)
            f(ga[:, :, :], gl[:, :, :], ACT.Exp).then_inc(gate_exp, 1)
            act.wait_ge(gate_step, 17)
            f(gs[:, 5, :], gs[:, 4, :], ACT.Exp).then_inc(gate_exp, 1)
            for c in each:
                arrived(act, ("s1", c))
                f(s1[:, c, :], ps(("s1", c)), ACT.Relu, bias=w("sb1")).then_inc(free(("s1", c)), 1)
            for c in each:
                arrived(act, ("s2a", c))
                f(s2[0][:, c, :], ps(("s2a", c)), ACT.Relu, bias=w("sb2")).then_inc(free(("s2a", c)), 1)
            for c in range(CHUNKS + 1):
                if c < CHUNKS:
                    if c >= 2:
                        arrived(act, ("e2", c - 2, 3))
                    for i in range(0, HALVES * EX, 2):
                        t = ("e1", c, i)
                        arrived(act, t)
                        f(hid[:, c % 2, i, :], ps(t), ACT.Relu, bias=w("eb1", i % EX, 1)).then_inc(free(t), 1)
                if c:
                    for i in range(4):
                        t = ("e2", c - 1, i)
                        arrived(act, t)
                        if c >= 3:
                            evacuated(act, ("g", c - 3, i))
                        f(e2[:, (c - 1) % 2, i, :], ps(t), ACT.Relu, bias=w("eb2", i % 2, 1)).then_inc(free(t), 1)

        @block.gpsimd
        def _(pool):
            pool.memset(eps[:, :], EPS).then_inc(constants, 1)
            for t in (x1, q, e, x2):
                pool.memset(t[:, :, CW:PADW], 0.0).then_inc(constants, 1)
            pool.memset(twice[:, :, :, :, TOK:D].rearrange("p c g i m -> p (c g i) m"), 0.0).then_inc(constants, 1)
            for t in (diag, pT):
                pool.memset(t[:, :, :, :, :], 0.0).then_inc(constants, 1)
            pool.memset(gp[:, :, :, :].bitcast(F32), 0.0).then_inc(constants, 1)
            for c in each:
                pool.wait_ge(h0_ready, c + 1)
                evacuated(pool, ("cen1", c))
                pool.tensor_tensor(h01[:, c, :], h0[:, c, :], x1[:, c, 0:CW], ALU.add).then_inc(h01_ready, 1)
            pool.wait_ge(w_loaded[1], 16)
            pool.tensor_copy(ident_b[:, :], w("ident")).then_inc(weights_split, 1)
            pool.tensor_copy(ident_r[:, :], w("ident")).then_inc(weights_split, 1)
            pool.wait_ge(w_loaded[2], 16)
            pool.tensor_copy(gsel[:, :, :], w("gsel").rearrange("p (i m) -> p i m", m=P)).then_inc(weights_split, 1)
            n = 3
            for name, dst in (("W1", w1s), ("eW1", e1s), ("eB3", b3s)):
                src = w(name)
                hi, lo = (dst[:, i].rearrange("p x m -> p (x m)") if len(dst.shape) == 4 else dst[:, i, :] for i in range(2))
                pool.tensor_copy(hi, src).then_inc(weights_split, 1)
                n += 1
                pool.wait_ge(weights_split, n)
                pool.tensor_tensor(lo, src, hi, ALU.subtract).then_inc(weights_split, 1)
                n += 1
            for name, dst in (("M1", m1s[:, :, :].rearrange("p i m -> p (i m)")), ("B2", b2s[:, :])):
                pool.wait_ge(weights_split, n)
                pool.tensor_copy(dst, w(name)).then_inc(weights_split, 1)
                n += 1
                pool.wait_ge(weights_split, n)
                pool.tensor_tensor(dst[half[1]], w(name, rows=half[1]), dst[half[1]], ALU.subtract)\
                    .then_inc(weights_split, 1)
                n += 1
            assert n == SPLITS
            pool.wait_ge(weights_split, n)
            for tile, x in (("cen2", x2), ("cen4", x4)):
                for c in each:
                    pool.wait_ge(xh_ready, (CHUNKS if tile == "cen4" else 0) + c + 1)
                    pool.tensor_tensor(xl[:, c % 2, :], x[:, c, 0:CW], xh[:, c % 2, :], ALU.subtract).then_inc(xl_ready, 1)

        @block.vector
        def _(dve):
            tt, ts, stt = nc.vector.tensor_tensor, nc.vector.tensor_scalar, nc.vector.scalar_tensor_tensor

            def across(column, n):
                return column.rearrange("p (g o) -> p g o", o=1).broadcast_to([column.shape[0], column.shape[1], n])

            def normalise(i, dst):
                for c in each:
                    dve.wait_ge(rstd_ready[i], c + 1)
                    t = (f"cen{i}", c)
                    tt(dst[:, c, 0:CW], ps(t), rstd[:, c, :], ALU.mult).then_inc(free(t), 1)

            arrived(dve, "setup")
            nc.vector.tensor_copy(tokW[:, :], bank[0][:, 0:2 * D + 1]).then_inc(free("setup"), 1)
            evacuated(dve, "setup")
            for c in each:
                dve.wait_ge(rstd_ready[0], c + 1)
                t = ("tok", c)
                stt(out=z[:, c, :], in0=ps(t), scalar=tokW[:, 2 * D:2 * D + 1], in1=rstd[:, c, :],
                    op0=ALU.add, op1=ALU.mult).then_inc(free(t), 1)
            normalise(1, x1)
            dve.wait_ge(w_loaded[1], 16)
            dve.wait_ge(constants, CONSTANTS)
            for c in each:
                arrived(dve, ("k", c))
                for h in range(HALVES):
                    last = ts(diag[half[h], c, :, h, :], ps(("k", c), half[h]).rearrange("p (b t) -> p b t", t=TOK),
                              w("bk", rows=half[h]), None, ALU.add)
                last.then_inc(free(("k", c)), 1)
            for c in each:
                arrived(dve, ("s", c))
                scores = ps(("s", c)).rearrange("p (b m) -> p b m", b=CB)
                nc.vector.reduce_max(mx[:, c, :], scores, AX.X).then_inc(max_ready, 1)
                dve.wait_ge(max_ready, c + 1)
                tt(e[:, c, 0:CW].rearrange("p (b m) -> p b m", b=CB), scores, across(mx[:, c, :], TOK), ALU.subtract)\
                    .then_inc(free(("s", c)), 1)
            for c in each:
                ec = e[:, c, 0:CW].rearrange("p (b m) -> p b m", b=CB)
                dve.wait_ge(e_ready, c + 1)
                nc.vector.reduce_sum(rsum[:, c, :], ec, AX.X).then_inc(sum_ready, 1)
                dve.wait_ge(sum_ready, c + 1)
                nc.vector.reciprocal(rinv[:, c, :], rsum[:, c, :]).then_inc(inv_ready, 1)
                dve.wait_ge(inv_ready, c + 1)
                tt(twice[:, c, :, :, 0:TOK],
                   e[:, c, 0:CW].rearrange("p (g o m) -> p g o m", o=1, m=TOK).broadcast_to([P, CB, 2, TOK]),
                   rinv[:, c, :].rearrange("p (g o q) -> p g o q", o=1, q=1).broadcast_to([P, CB, 2, TOK]),
                   ALU.mult).then_inc(p_ready, 1)
            for c in each:
                arrived(dve, ("ptb", c))
                for s in range(2):
                    rows = slice(D * s, D * s + TOK)
                    last = nc.vector.tensor_copy(
                        pT[rows, c, 4:8, s, :],
                        bank[plan[("ptb", c)][0]][rows, :].rearrange("p (g s n) -> p g s n", s=2, n=D)[:, :, s, 0:TOK])
                last.then_inc(free(("ptb", c)), 1)
            for c in each:
                arrived(dve, ("pv", c))
                ts(at[:, c, :], ps(("pv", c)), w("bv"), None, ALU.add).then_inc(free(("pv", c)), 1)
            for c in each:
                evacuated(dve, ("wl", c))
                nc.vector.bn_stats(stats[:, c, :], hl[:, c, 0:CW]).then_inc(stats_ready, 1)
            dve.wait_ge(stats_ready, CHUNKS)
            nc.vector.bn_aggr(bn[:, 0:2], stats[:, :, :]).then_inc(bn_step, 1)
            arrived(dve, "bn1")
            nc.vector.tensor_copy(bn[:, 2:4], ps("bn1", n=2)).then_inc(free("bn1"), 1)
            evacuated(dve, "bn1")
            tt(bn[:, 4:5], bn[:, 0:1], bn[:, 2:3], ALU.subtract).then_inc(bn_step, 1)
            dve.wait_ge(bn_step, 2)
            tt(bn[:, 5:6], bn[:, 4:5], bn[:, 4:5], ALU.mult).then_inc(bn_step, 1)
            arrived(dve, "bn2")
            tt(bn[:, 6:7], ps("bn2", n=1), bn[:, 3:4], ALU.add).then_inc(free("bn2"), 1)
            dve.wait_ge(bn_rstd, 1)
            tt(bn[:, 9:10], bn[:, 8:9], w("bng"), ALU.mult).then_inc(bn_step, 1)
            dve.wait_ge(bn_step, 4)
            tt(bn[:, 10:11], bn[:, 2:3], bn[:, 9:10], ALU.mult).then_inc(bn_step, 1)
            dve.wait_ge(bn_step, 5)
            tt(bn[:, 11:12], w("bnb"), bn[:, 10:11], ALU.subtract).then_inc(bn_step, 1)
            for c in each:
                dve.wait_ge(y_ready, c + 1)
                dve.wait_ge(h01_ready, c + 1)
                tt(h1[:, c, :], h01[:, c, :], hl[:, c, 0:CW], ALU.add).then_inc(h1_ready, 1)
            normalise(2, x2)
            dve.wait_ge(w_loaded[2], 16)
            for c in each:
                t = ("lg", c)
                n = c * 4
                arrived(dve, t)
                tt(lg[:, :, :].rearrange("p (u h) e -> p u (h e)", u=NT),
                   ps(t, n=NT * HALVES * NE).rearrange("p (u g) -> p u g", u=NT),
                   w("routerb").rearrange("p (o g) -> p o g", o=1).broadcast_to([P, NT, HALVES * NE]),
                   ALU.add).then_inc(free(t), 1)
                evacuated(dve, t)
                nc.vector.reduce_max(lmx[:, :], lg[:, :, :], AX.X).then_inc(route_step, 1)
                dve.wait_ge(route_step, n + 1)
                tt(first[:, :, :], lg[:, :, :], across(lmx[:, :], NE), ALU.is_equal).then_inc(route_step, 1)
                dve.wait_ge(route_step, n + 2)
                tt(first[:, :, :].rearrange("p (u h) e -> p u (h e)", u=NT),
                   first[:, :, :].rearrange("p (u h) e -> p u (h e)", u=NT),
                   w("rank").rearrange("p (o g) -> p o g", o=1).broadcast_to([P, NT, HALVES * NE]),
                   ALU.mult).then_inc(route_step, 1)
                dve.wait_ge(route_step, n + 3)
                nc.vector.reduce_max(lmx[:, :], first[:, :, :], AX.X).then_inc(route_step, 1)
                dve.wait_ge(route_step, n + 4)
                if c >= 2:
                    arrived(dve, ("oh", c - 2))
                for i in range(2):
                    last = tt(onehot[:, c % 2, :, i, :].rearrange("p u (h e) -> p u h e", h=HALVES),
                              first[:, :, :].rearrange("p (u h) e -> p u h e", u=NT),
                              lmx[:, :].rearrange("p (u h o) -> p u h o", u=NT, o=1).broadcast_to([P, NT, HALVES, NE]),
                              ALU.is_equal)
                last.then_inc(oh_ready, 1)
                if c:
                    t = ("oh", c - 1)
                    arrived(dve, t)
                    nc.vector.tensor_copy(ohT[:, c - 1, :], ps(t)).then_inc(free(t), 1)
            t = ("oh", CHUNKS - 1)
            arrived(dve, t)
            nc.vector.tensor_copy(ohT[:, CHUNKS - 1, :], ps(t)).then_inc(free(t), 1)
            for c in range(CHUNKS + 1):
                if c < CHUNKS:
                    if c >= 2:
                        arrived(dve, ("moe", c - 2))
                    for i in range(1, HALVES * MT, 2):
                        t = ("hid", c, i)
                        arrived(dve, t)
                        ts(hid[:, c % 2, i, :], ps(t), 0.0, None, ALU.max).then_inc(free(t), 1)
                if c:
                    t = ("moe", c - 1)
                    arrived(dve, t)
                    stt(out=h2[:, c - 1, :], in0=ps(t), scalar=0.0, in1=h1[:, c - 1, :],
                        op0=ALU.max, op1=ALU.add).then_inc(free(t), 1)
            normalise(3, x3)
            for c in each:
                t = ("v3", c)
                arrived(dve, t)
                tt(v[:, c].rearrange("p j h d -> p (j h d)"), ps(t, n=CB * D), w("vb"), ALU.add).then_inc(free(t), 1)
            for c in each:
                for n, folded, dst in (("k2", k_folded, kf), ("q2", q_folded, qf)):
                    evacuated(dve, (n, c))
                    stt(out=dst[:, c, 0:CW], in0=dst[:, c, 0:CW], scalar=w("fold"), in1=dst[:, c, 0:CW],
                        op0=ALU.mult, op1=ALU.max).then_inc(folded, 1)
            for c in each:
                t = ("st", c)
                arrived(dve, t)
                for s in range(2):
                    rows = slice(D * s, D * s + TOK)
                    last = tt(pT[rows, c, :, s, :], ps(t, rows).rearrange("p (g n) -> p g n", n=TOK),
                              w("causal", rows=rows).rearrange("p (o n) -> p o n", o=1).broadcast_to([TOK, CB, TOK]),
                              ALU.mult)
                last.then_inc(free(t), 1)
            for c in each:
                t = ("ret", c)
                arrived(dve, t)
                tt(h3[:, c, :], ps(t), h2[:, c, :], ALU.add).then_inc(free(t), 1)
            normalise(4, x4)
            arrived(dve, "gate")
            G = slice(0, P)
            tt(gl[G].rearrange("p (t h) e -> p t (h e)", h=HALVES),
               ps("gate", G, GT * EX).rearrange("p (t g) -> p t g", g=HALVES * EX),
               w("gb", rows=G).rearrange("p (o g) -> p o g", o=1).broadcast_to([P, GT // HALVES, HALVES * EX]),
               ALU.add).then_inc(free("gate"), 1)
            evacuated(dve, "gate")
            rank = w("grank", 0, EX, G).rearrange("p (o e) -> p o e", o=1).broadcast_to([P, GT, EX])
            nc.vector.reduce_max(gs[G, 0, :], gl[G], AX.X).then_inc(gate_step, 1)
            dve.wait_ge(gate_step, 1)
            tt(gl[G], gl[G], across(gs[G, 0, :], EX), ALU.subtract).then_inc(gate_step, 1)
            dve.wait_ge(gate_exp, 1)
            nc.vector.reduce_sum(gs[G, 1, :], ga[G], AX.X).then_inc(gate_step, 1)
            dve.wait_ge(gate_step, 3)
            nc.vector.reciprocal(gs[G, 2, :], gs[G, 1, :]).then_inc(gate_step, 1)
            dve.wait_ge(gate_step, 4)
            tt(ga[G], ga[G], across(gs[G, 2, :], EX), ALU.mult).then_inc(gate_step, 1)
            dve.wait_ge(gate_step, 5)
            nc.vector.reduce_max(gs[G, 0, :], ga[G], AX.X).then_inc(gate_step, 1)
            dve.wait_ge(gate_step, 6)
            tt(gc[G], ga[G], across(gs[G, 0, :], EX), ALU.is_equal).then_inc(gate_step, 1)
            dve.wait_ge(gate_step, 7)
            tt(gc[G], gc[G], rank, ALU.mult).then_inc(gate_step, 1)
            dve.wait_ge(gate_step, 8)
            nc.vector.reduce_max(gs[G, 3, :], gc[G], AX.X).then_inc(gate_step, 1)
            dve.wait_ge(gate_step, 9)
            tt(gm1[G], gc[G], across(gs[G, 3, :], EX), ALU.is_equal).then_inc(gate_step, 1)
            dve.wait_ge(gate_step, 10)
            stt(out=gl[G], in0=gm1[G], scalar=-2.0, in1=ga[G], op0=ALU.mult, op1=ALU.add).then_inc(gate_step, 1)
            dve.wait_ge(gate_step, 11)
            nc.vector.reduce_max(gs[G, 1, :], gl[G], AX.X).then_inc(gate_step, 1)
            dve.wait_ge(gate_step, 12)
            tt(gc[G], gl[G], across(gs[G, 1, :], EX), ALU.is_equal).then_inc(gate_step, 1)
            dve.wait_ge(gate_step, 13)
            tt(gc[G], gc[G], rank, ALU.mult).then_inc(gate_step, 1)
            dve.wait_ge(gate_step, 14)
            nc.vector.reduce_max(gs[G, 3, :], gc[G], AX.X).then_inc(gate_step, 1)
            dve.wait_ge(gate_step, 15)
            tt(gm2[G], gc[G], across(gs[G, 3, :], EX), ALU.is_equal).then_inc(gate_step, 1)
            tt(gs[G, 4, :], gs[G, 1, :], gs[G, 0, :], ALU.subtract).then_inc(gate_step, 1)
            dve.wait_ge(gate_exp, 2)
            ts(gs[G, 6, :], gs[G, 5, :], 1.0, None, ALU.add).then_inc(gate_step, 1)
            dve.wait_ge(gate_step, 18)
            nc.vector.reciprocal(gs[G, 2, :], gs[G, 6, :]).then_inc(gate_step, 1)
            dve.wait_ge(gate_step, 19)
            tt(gs[G, 7, :], gs[G, 5, :], gs[G, 2, :], ALU.mult).then_inc(gate_step, 1)
            tt(gm1[G], gm1[G], across(gs[G, 2, :], EX), ALU.mult).then_inc(gate_step, 1)
            dve.wait_ge(gate_step, 20)
            tt(gm2[G], gm2[G], across(gs[G, 7, :], EX), ALU.mult).then_inc(gate_step, 1)
            dve.wait_ge(gate_step, 22)
            tt(gsum[G], gm1[G], gm2[G], ALU.add).then_inc(gate_step, 1)
            dve.wait_ge(gate_step, 23)
            gates = gsum[:, :, :].rearrange("p (t h) e -> p t (h e)", h=HALVES)
            hi, lo = (gp[:, :, :, i * HALVES * EX:(i + 1) * HALVES * EX].rearrange("p c u g -> p (c u) g") for i in range(2))
            nc.vector.tensor_copy(hi, gates).then_inc(gate_step, 1)
            dve.wait_ge(gate_step, 24)
            tt(lo, gates, hi, ALU.subtract).then_inc(gp_ready, 1)
            for c in each:
                t = ("s2b", c)
                arrived(dve, t)
                ts(s2[1][:, c, :], ps(t), w("sb2"), 0.0, ALU.add, ALU.max).then_inc(free(t), 1)
            for c in range(CHUNKS + 1):
                if c < CHUNKS:
                    if c >= 2:
                        arrived(dve, ("e2", c - 2, 3))
                    for i in range(1, HALVES * EX, 2):
                        t = ("e1", c, i)
                        arrived(dve, t)
                        ts(hid[:, c % 2, i, :], ps(t), w("eb1", i % EX, 1), 0.0, ALU.add, ALU.max)\
                            .then_inc(free(t), 1)
                    t = ("gt", c)
                    arrived(dve, t)
                    nc.vector.tensor_copy(gT[:, c, :], ps(t)).then_inc(free(t), 1)
                if c:
                    for i in range(4):
                        t = ("g", c - 1, i)
                        arrived(dve, t)
                        evacuated(dve, ("e2", c - 1, i))
                        tt(ge[:, (c - 1) % 2, i, :], ps(t), e2[:, (c - 1) % 2, i, :], ALU.mult).then_inc(free(t), 1)
                    t = ("fin", c - 1)
                    arrived(dve, t)
                    stt(out=res[:, c - 1, :], in0=ps(t), scalar=w("sb3"), in1=h3[:, c - 1, :],
                        op0=ALU.add, op1=ALU.add).then_inc(free(t), 1)


def pack_weights(a):
    pack = np.zeros((P, PACKW), np.float32)

    def put(name, block, row=0, lo=0):
        pack[row:row + block.shape[0], COL[name] + lo:COL[name] + lo + block.shape[1]] = block

    def both(name, block):
        for h in range(HALVES):
            put(name, block, D * h, block.shape[1] * h)

    def column(name, vec, lo=0):
        for r in range(0, P, len(vec)):
            put(name, vec[:, None], r, lo)

    eye = np.eye(D, dtype=np.float32)
    ones = np.ones((D, D), np.float32)
    put("tokW", a["L0_tok_W"])
    both("center", eye - np.float32(1.0 / D) * ones)
    both("mean", np.float32(1.0 / D) * ones)
    column("tokb", a["L0_tok_b"])
    column("tokg", a["L0_tok_gamma"])
    column("tokbeta", a["L0_tok_beta"])
    for n in "qkvl":
        both("W" + n, a["L0_attn_W" + n])
        column("b" + n, a["L0_attn_b" + n])
    column("bng", a["L0_attn_gamma"])
    column("bnb", a["L0_attn_beta"])
    pack[:, COL["avg"]:COL["avg"] + P] = np.tile(np.float32(0.5) * eye, (2, 2))
    put("ident", np.eye(P, dtype=np.float32))
    both("router", a["L0_ffn_router_w"].T)
    put("routerb", np.tile(a["L0_ffn_router_b"], (P, HALVES)))
    put("rank", np.tile(np.arange(NE, 0, -1, dtype=np.float32), (P, HALVES)))
    w1 = a["L0_ffn_W1"].transpose(1, 0, 2).reshape(D, NE * NH)
    own = np.full((NE, NE, NH), -BIG, np.float32)
    own[np.arange(NE), np.arange(NE)] = a["L0_ffn_b1"]
    w2 = a["L0_ffn_W2"].reshape(NE * NH, D)
    for h in range(HALVES):
        put("W1", w1, D * h)
        for r in range(0, P, HALVES * NE):
            put("M1", own.reshape(NE, NE * NH), r + NE * h, h * MT * P)
            put("B2", a["L0_ffn_b2"], r + NE * h, h * D)
    for m in range(MT):
        put("W2", w2[m * P:m * P + P], 0, m * D)
    for n in "kq":
        both(n + "w1", a[f"L1_attn_{n}w1"].T)
        both(n + "w2", np.tile(a[f"L1_attn_{n}w2"].T, (1, 2)))
        column(n + "b1", a[f"L1_attn_{n}b1"])
        column(n + "b2", a[f"L1_attn_{n}b2"])
    both("vw", a["L1_attn_vw"].T)
    put("vb", np.tile(a["L1_attn_vb"], (P, CB)))
    m, n = np.arange(P)[:, None] % D, np.arange(TOK)[None]
    put("causal", np.where(m <= n, 1.0 / np.sqrt((n + 1.0) * KP), 0.0).astype(np.float32))
    cosine = (np.arange(P) % D < KP)
    column("fold", np.where(cosine, -1.0, 1.0).astype(np.float32))
    column("sscale", np.where(cosine, -np.pi, np.pi).astype(np.float32))
    column("sbias", np.where(cosine, np.pi / 2, 0.0).astype(np.float32))
    both("gW", a["L1_ffn_gW"])
    put("gb", np.tile(a["L1_ffn_gb"], (P, HALVES)))
    put("grank", np.tile(np.arange(EX, 0, -1, dtype=np.float32), (P, HALVES)))
    both("sW1", a["L1_ffn_sW1"])
    put("sW3", a["L1_ffn_sW3"])
    column("sb1", a["L1_ffn_sb1"])
    column("sb2", a["L1_ffn_sb2"])
    column("sb3", a["L1_ffn_sb3"])
    for h in range(HALVES):
        put("sW2", a["L1_ffn_sW2"], D * h, h * P)
        for x in range(EX):
            put("eW1", a["L1_ffn_eW1"][x], D * h, x * P)
            pair, j = x // 2, x % 2
            for r in (0, HALVES * EX):
                put("gsel", np.ones((1, D), np.float32), r + h * EX + x, (2 * h + pair) * P + j * D)
        for r in (0, HALVES * EX):
            put("eB3", a["L1_ffn_eb3"], r + EX * h, h * D)
    for x in range(EX):
        put("eW2", a["L1_ffn_eW2"][x], 0, x * D)
        put("eW3", a["L1_ffn_eW3"][x], D * (x % 2), (x // 2) * D)
        column("eb1", a["L1_ffn_eb1"][x], x)
        put("eb2", a["L1_ffn_eb2"][x][:, None], D * (x % 2), x // 2)
    return pack


def kernel(**inputs):
    import concourse.bacc as bacc
    from concourse.bass_utils import run_bass_kernel_spmd

    a = {n: np.asarray(x) for n, x in inputs.items()}
    x = a["x"][:, :BLOCKS * STRIDE].reshape(HALVES, CHUNKS, CB, BLOCKS, STRIDE * FEAT)
    arrays = {"xblk": np.ascontiguousarray(x.transpose(4, 1, 0, 2, 3)), "wpack": pack_weights(a)}
    nc = bacc.Bacc("TRN2", target_bir_lowering=False, num_devices=1)
    args = [nc.dram_tensor(n, v.shape, F32, kind="ExternalInput").ap() for n, v in arrays.items()]
    out = nc.dram_tensor("out", (P, CHUNKS, CW), F32, kind="ExternalOutput").ap()
    audio_tower_kernel(nc, *args, out)
    r = run_bass_kernel_spmd(nc, [arrays], core_ids=[0])
    o = r.results[0]["out"].reshape(HALVES, D, CHUNKS, CB, TOK)
    return np.ascontiguousarray(o.transpose(0, 2, 3, 4, 1)).reshape(B, TOK, D)
```

```python
from contextlib import ExitStack

import numpy as np
import concourse.bass as bass
from concourse import mybir

B, SEQ, FEAT = 64, 375, 16
PATCH, STRIDE, D = 16, 8, 64
TOK = (SEQ - PATCH) // STRIDE + 1
BLOCKS = TOK + PATCH // STRIDE - 1
P = 128
HALVES = P // D
HB = B // HALVES
CHUNKS = 4
CB = HB // CHUNKS
CW = CB * TOK
PADW = CW + D - TOK
CJ = CB // 2
TT = 60
NT = CW // (2 * TT)
NE, NH = 32, 16
MT = NE * NH // P
KP = 32
SH1, SH2, EH1, EH2, EX = 64, 128, 128, 64, 4
BANKS = 8
BIG = 2.0 ** 100
EPS = 1e-5
PI = float(np.float32(np.pi))

F32 = mybir.dt.float32
F32R = mybir.dt.float32r
BF16 = mybir.dt.bfloat16
ALU = mybir.AluOpType
ACT = mybir.ActivationFunctionType
LN_EXP = "natural_log_exp_and_others"
AX = mybir.AxisListType

PACK = [
    ("tokW", P), ("center", P), ("tokb", 1), ("tokg", 1), ("tokbeta", 1),
    ("mean", P), ("Wq", P), ("Wk", P), ("Wv", P), ("Wl", P), ("bq", 1), ("bk", 1), ("bv", 1), ("bl", 1),
    ("bng", 1), ("bnb", 1), ("avg", P), ("ident", P),
    ("router", HALVES * NE), ("routerb", HALVES * NE), ("rank", HALVES * NE),
    ("W1", MT * P), ("M1", MT * P), ("W2", MT * D), ("B2", HALVES * P),
    ("kw1", P), ("qw1", P), ("kw2", P), ("qw2", P), ("vw", P), ("vb", CB * D), ("causal", TOK),
    ("kb1", 1), ("qb1", 1), ("kb2", 1), ("qb2", 1), ("fold", 1), ("sbias", 1),
    ("gW", HALVES * EX), ("gb", HALVES * EX), ("grank", HALVES * EX),
    ("sW1", P), ("sW2", HALVES * P), ("sW3", D), ("eW1", EX * P), ("eW2", EX * D),
    ("eW3", 2 * D), ("eB3", P), ("gsel", HALVES * 2 * P),
    ("sb1", 1), ("sb2", 1), ("sb3", 1), ("eb1", EX), ("eb2", 2),
]
COL, WIDTH = {}, dict(PACK)
_at = 0
for _n, _w in PACK:
    COL[_n] = _at
    _at += _w
PACKW = _at
CUT1 = COL["mean"]
CUT2 = COL["router"]

HID_ACT = ((0, 1, 2, 3, 4, 5, 6), *[(0, 1, 3, 5, 6)] * 3)
GT_AT, GATES_IN = 3, ((), (0, 1), (2,), (3,))
E1_ACT = ((0, 1, 3, 4, 5, 7), (0, 2, 4, 6), (0, 2, 4, 6), (0, 2, 4, 6))
RELU_ACT = 2
LG_BEHIND, LG_AT = 3, 1
EXP2_AT = 3
BN_AFTER = 1
OH_AT = 4
AHEAD = 2


def live(c):
    return 0 <= c < CHUNKS


def psum_plan():
    plan, uses, drains, release, count = {}, [0] * BANKS, [0] * BANKS, [0] * BANKS, 0
    readers = {"k": 2}

    def fill(tile, hold=8):
        nonlocal count
        b = release.index(min(release))
        after = drains[b] + readers.get(tile[0], 1)
        plan[tile] = (b, uses[b], drains[b], after)
        uses[b] += 1
        drains[b] = after
        release[b] = count + hold
        count += 1

    fill("setup", 1)
    for s in range(CHUNKS + 9):
        for tile, behind, hold in (("tok", 0, 12), ("var0", 1, 4), ("cen1", 2, 12), ("var1", 3, 4), ("q", 4, 4),
                                   ("k", 4, 5), ("s", 5, 7), ("v", 5, 5), ("pta", 7, 5), ("ptb", 7, 5),
                                   ("pv", 8, 5), ("wl", 9, 5)):
            if live(s - behind):
                fill((tile, s - behind), hold)
    for c in range(CHUNKS):
        if c == BN_AFTER:
            fill("bn1", 4)
        fill(("cen2", c), 12)
    for s in range(CHUNKS + 4):
        for tile, behind, hold in (("lg", LG_BEHIND, 7), ("var2", 1, 3)):
            if live(s - behind) and (tile, s - behind) != ("lg", CHUNKS - 1):
                fill((tile, s - behind), hold)
    for c in range(CHUNKS + 6):
        if live(c):
            for i in range(HALVES * MT):
                if c == 0 and i == 0:
                    fill(("oh", 0, 0), 4), fill(("oh", 0, 1), 4)
                fill(("hid", c, i))
                if c == 0 and i == max(LG_AT, AHEAD - 1):
                    fill(("lg", CHUNKS - 1), 7)
                if i == OH_AT and live(c + 1):
                    fill(("oh", c + 1, 0), 6), fill(("oh", c + 1, 1), 6)
        if live(c - 1):
            fill(("moe", c - 1), 6)
        if live(c - 2):
            fill(("cen3", c - 2), 16)
        if live(c - 3):
            fill(("var3", c - 3), 4)
        if live(c - 6):
            fill(("q1", c - 6), 6)
        if live(c - 5):
            fill(("k1", c - 5), 6)
        if c == 7:
            fill(("v3", 0), 5)
    for c in range(CHUNKS):
        fill(("k2", c)), fill(("q2", c))
    for c in range(1, CHUNKS):
        fill(("v3", c), 5)
    for s in range(CHUNKS + 4):
        for tile, behind, hold in (("st", 0, 4), ("ret", 1, 4), ("cen4", 2, 9), ("var4", 3, 3), ("s1", 4, 4)):
            if tile == "s1" and s == 4:
                fill("gate", 12)
            if live(s - behind):
                fill((tile, s - behind), hold)
    for c in range(CHUNKS):
        fill(("s2a", c)), fill(("s2b", c))
    for c in range(CHUNKS + 1):
        if live(c):
            for i in range(HALVES * EX):
                fill(("e1", c, i))
                if i == GT_AT:
                    for g in GATES_IN[c]:
                        fill(("gt", g), 8)
        if c:
            for i in (0, 2):
                fill(("e2", c - 1, i)), fill(("e2", c - 1, i + 1)), fill(("g", c - 1, i)), fill(("g", c - 1, i + 1))
            fill(("fin", c - 1))
    return plan


def audio_tower_kernel(nc, xblk, wpack, out):
    plan = psum_plan()
    each = range(CHUNKS)
    with ExitStack() as ctx:
        def sb(name, *free, dt=F32):
            return ctx.enter_context(nc.sbuf_tensor(name, [P, *free], dt))

        def sem(name):
            return ctx.enter_context(nc.semaphore(name))

        bank = [ctx.enter_context(nc.psum_tensor(f"bank{i}", [P, 512], F32)) for i in range(BANKS)]
        filled = [sem(f"filled{i}") for i in range(BANKS)]
        drained = [sem(f"drained{i}") for i in range(BANKS)]

        GT = CHUNKS * NT * HALVES
        W = sb("W", PACKW)
        X = sb("X", CHUNKS, HALVES, CB, BLOCKS)
        tokW = sb("tokW_centred", 2 * D + 1)
        eps = sb("eps", 1)
        sq = sb("sq", CHUNKS, CW)
        lnv = sb("lnv", CHUNKS, CW)
        rstd = sb("rstd", CHUNKS, CW)
        z = sb("z", CHUNKS, CW)
        h0 = sb("h0", CHUNKS, CW)
        x1 = sb("x1", CHUNKS, PADW)
        q = sb("q", CHUNKS, PADW)
        diag = sb("diag", CHUNKS, CB, HALVES, TOK)
        v = sb("v", CHUNKS, CJ, HALVES, D)
        mx = sb("mx", CHUNKS, CB)
        e = sb("e", CHUNKS, PADW)
        rsum = sb("rsum", CHUNKS, CB)
        rinv = sb("rinv", CHUNKS, CB)
        pT = sb("pT", CHUNKS, CB, 2, TOK)
        stats = sb("stats", CHUNKS, 6)
        bn = sb("bn", 12)
        h01 = sb("h01", CHUNKS, CW)
        x2 = sb("x2", CHUNKS, PADW)
        lmx = sb("lmx", CHUNKS, NT * HALVES)
        first = sb("first", CHUNKS, NT * HALVES, NE)
        onehot = sb("onehot", 2, NT, HALVES, 2, NE, dt=BF16)
        xs = sb("xs", 2, HALVES, CHUNKS, CW, dt=F32R)
        ident_b = sb("ident_b", P, dt=BF16)
        ident_r = sb("ident_r", P, dt=F32R)
        w1s = sb("w1s", 2, MT, P, dt=F32R)
        e1s = sb("e1s", 2, EX, P, dt=F32R)
        center_r = sb("center_r", P, dt=F32R)
        b2s = sb("b2s", HALVES, P, dt=F32R)
        b3s = sb("b3s", P, dt=F32R)
        gsel = sb("gsel", 4, P, dt=F32R)
        hid = sb("hid", 2, HALVES * MT, CW)
        gl = sb("gl", GT, EX)
        ga = sb("ga", GT, EX)
        gc = sb("gc", GT, EX)
        gm1 = sb("gm1", GT, EX)
        gm2 = sb("gm2", GT, EX)
        gs = sb("gs", 8, GT)
        gsum = sb("gsum", GT, EX)
        gp = sb("gp", CHUNKS, NT, P, dt=F32R)
        at, hl, x3 = z, q, x2
        xh, xl = (t[:, :, 0:CW].bitcast(F32R) for t in (e, q))
        lg = z[:, :, :].rearrange("p c n -> p (c n)")[:, 0:CHUNKS * NT * HALVES * NE].rearrange(
            "p (c g e) -> p c g e", c=CHUNKS, e=NE)
        hh, hlo = xs[:, 0, 0], xs[:, 0, 1]
        twice = hid[:, :, :, :].rearrange("p u i n -> p (u i n)")[:, 0:CHUNKS * CB * 2 * D].rearrange(
            "p (c g i m) -> p c g i m", c=CHUNKS, g=CB, i=2)
        k1, kf, q1, qf = x1, x1, e, e
        spent = X[:, :, :, :, :].rearrange("p c h b t -> p (c h b t)")[:, 0:2 * CHUNKS * CW]
        h1, h2 = (spent[:, i * CHUNKS * CW:(i + 1) * CHUNKS * CW].rearrange("p (c n) -> p c n", n=CW) for i in range(2))
        h3, x4, s1, s2, gT, res = h1, x1, z, (h0, h01), xs[:, 1, 0], h2
        ge = pT[:, :, :, :, :].rearrange("p c b h t -> p (c b h t)").rearrange("p (u i n) -> p u i n", u=2, i=4)
        e2 = diag[:, :, :, :, :].rearrange("p c b h t -> p (c b h t)").rearrange("p (u i n) -> p u i n", u=2, i=4)

        def w(name, lo=0, n=None, rows=slice(0, P)):
            n = WIDTH[name] if n is None else n
            return W[rows, COL[name] + lo:COL[name] + lo + n]

        x_loaded = [sem(f"x_loaded{c}") for c in each]
        w_loaded = [sem(f"w_loaded{i}") for i in range(3)]
        out_stored = sem("out_stored")
        CONSTANTS = 9
        constants = sem("constants")
        sq_ready = [sem(f"sq_ready{i}") for i in range(5)]
        ln_ready = [sem(f"ln_ready{i}") for i in range(5)]
        rstd_ready = [sem(f"rstd_ready{i}") for i in range(5)]
        y_step, y2_ready, h0_ready, h01_ready, h1_ready = (sem(n) for n in ("y_step", "y2_ready", "h0_ready", "h01_ready", "h1_ready"))
        max_ready, e_ready, sum_ready = sem("max_ready"), sem("e_ready"), sem("sum_ready")
        inv_ready = sem("inv_ready")
        p_ready = [sem(f"p{i}_ready") for i in range(2)]
        stats_ready, bn_step, bn_rstd, y_ready = (sem(n) for n in ("stats_ready", "bn_step", "bn_rstd", "y_ready"))
        route_step, oh_ready = [sem(f"route_step{c}") for c in each], sem("oh_ready")
        k_folded, q_folded, kf_ready, qf_ready = (sem(n) for n in ("k_folded", "q_folded", "kf_ready", "qf_ready"))
        weights_split, SPLITS1, SPLITS = sem("weights_split"), 7, 14
        xh_ready = sem("xh_ready")
        xl_ready = [sem(f"xl_ready{c}") for c in each]
        split_moved = [sem(f"split_moved{c}") for c in each]
        hh_ready, hlo_ready = sem("hh_ready"), sem("hlo_ready")
        gate_step, gate_exp, gp_ready = ([sem(f"{n}{g}") for g in range(2)] for n in ("gate_step", "gate_exp", "gp_ready"))

        def ps(tile, rows=slice(0, P), n=CW):
            return bank[plan[tile][0]][rows, 0:n]

        def claim(pe, tile):
            b, use, before, _ = plan[tile]
            if use:
                pe.wait_ge(drained[b], before)

        def full(tile):
            return filled[plan[tile][0]]

        def arrived(eng, tile):
            b, use, _, _ = plan[tile]
            eng.wait_ge(filled[b], use + 1)

        def free(tile):
            return drained[plan[tile][0]]

        def evacuated(eng, tile):
            b, _, _, after = plan[tile]
            eng.wait_ge(drained[b], after)

        def y_wait(eng, c):
            eng.wait_ge(*((y_ready, c + 1) if c < RELU_ACT else (y2_ready, c - RELU_ACT + 1)))

        half = [slice(D * h, D * h + D) for h in range(HALVES)]
        block = ctx.enter_context(nc.Block())

        @block.sync
        def _(sp):
            sp.dma_start(W[:, 0:CUT1], wpack[:, 0:CUT1]).then_inc(w_loaded[0], 16)
            sp.dma_start(W[:, CUT1:CUT2], wpack[:, CUT1:CUT2]).then_inc(w_loaded[1], 16)
            for c in range(1, CHUNKS):
                sp.dma_start(X[:, c], xblk[:, c]).then_inc(x_loaded[c], 16)
            sp.dma_start(W[:, CUT2:PACKW], wpack[:, CUT2:PACKW]).then_inc(w_loaded[2], 16)
            for r in range(2):
                for c in each:
                    n = CHUNKS * r + c
                    if r:
                        arrived(sp, ("hid", c, HALVES * MT - 1))
                    for part, src, ready, count in ((0, xh, xh_ready, n + 1), (1, xl, xl_ready[c], r + 1)):
                        sp.wait_ge(ready, count)
                        for h in range(HALVES):
                            copies = 2 if r == 0 and part == 0 else 1
                            sp.dma_start(xs[half[part], 0:copies, h, c, :].bitcast(F32),
                                         src[half[h], c, :].bitcast(F32).rearrange("p (i n) -> p i n", i=1)
                                         .broadcast_to([D, copies, CW])).then_inc(split_moved[c], 16)
            for c in each:
                evacuated(sp, ("fin", c))
                sp.dma_start(out[:, c], res[:, c, :]).then_inc(out_stored, 16)
            sp.wait_ge(out_stored, 16 * CHUNKS)

        @block.tensor
        def _(pe):
            mm = nc.tensor.matmul

            def centre(i, src, c):
                t = (f"cen{i}", c)
                claim(pe, t)
                mm(ps(t), w("center"), src[:, c, 0:CW], start=True, stop=True).then_inc(full(t), 1)

            def centre_parts(i, c):
                t = (f"cen{i}", c)
                pe.wait_ge(weights_split, SPLITS)
                pe.wait_ge(hlo_ready, c + 1)
                claim(pe, t)
                mm(ps(t), center_r[:, :], hh[:, c, :], start=True, stop=False)
                mm(ps(t), center_r[:, :], hlo[:, c, :], start=False, stop=True).then_inc(full(t), 1)

            def variance(i, c):
                pe.wait_ge(sq_ready[i], c + 1)
                t = (f"var{i}", c)
                claim(pe, t)
                mm(ps(t), w("mean"), sq[:, c, :], start=True, stop=True).then_inc(full(t), 1)

            def values(t, x, weight):
                claim(pe, t)
                c = t[1]
                for b in range(CB):
                    j, s = b // 2, b % 2
                    last = mm(bank[plan[t][0]][half[s], j * P:j * P + P], x[:, c, b * TOK:b * TOK + D],
                              w(weight), start=True, stop=True)
                last.then_inc(full(t), 1)

            def products(t, stationary, diagonal):
                claim(pe, t)
                c = t[1]
                for b in range(CB):
                    j, s = b // 2, b % 2
                    last = mm(bank[plan[t][0]][half[s], 2 * j * TOK:2 * (j + 1) * TOK],
                              stationary[:, c, b * TOK:b * TOK + D], diagonal[:, c, b, :, :], start=True, stop=True)
                last.then_inc(full(t), 1)

            def weighted_values(t, pairs):
                claim(pe, t)
                c = t[1]
                for j in range(CJ):
                    for h in range(HALVES):
                        last = mm(bank[plan[t][0]][half[h], 2 * j * TOK:2 * (j + 1) * TOK],
                                  v[:, c, j, h, :], pairs[:, c, HALVES * j + h, :, :], start=True, stop=True)
                last.then_inc(full(t), 1)

            pe.wait_ge(w_loaded[0], 16)
            mm(bank[0][:, 0:2 * D], w("tokW"), w("center"), start=True, stop=True)
            mm(bank[0][:, 2 * D:2 * D + 1], w("center"), w("tokb"), start=True, stop=True).then_inc(full("setup"), 1)
            evacuated(pe, "setup")
            for s in range(CHUNKS + 9):
                if live(s):
                    pe.wait_ge(x_loaded[s], 16)
                    claim(pe, ("tok", s))
                    for i in range(2):
                        for h in range(HALVES):
                            last = mm(ps(("tok", s), half[h]), tokW[:, i * D:i * D + D], X[:, s, h, :, i:i + TOK],
                                      start=(i == 0), stop=(i == 1))
                    last.then_inc(full(("tok", s)), 1)
                if live(s - 1):
                    pe.wait_ge(w_loaded[1], 16)
                    variance(0, s - 1)
                if live(s - 2):
                    pe.wait_ge(h0_ready, s - 1)
                    centre(1, h0, s - 2)
                if live(s - 3):
                    variance(1, s - 3)
                if live(s - 4):
                    c = s - 4
                    pe.wait_ge(w_loaded[1], 16)
                    evacuated(pe, ("cen1", c))
                    for n, wn in (("q", "Wq"), ("k", "Wk")):
                        claim(pe, (n, c))
                        mm(ps((n, c)), w(wn), x1[:, c, 0:CW], start=True, stop=True).then_inc(full((n, c)), 1)
                if live(s - 5):
                    c = s - 5
                    pe.wait_ge(constants, CONSTANTS)
                    evacuated(pe, ("q", c))
                    evacuated(pe, ("k", c))
                    products(("s", c), q, diag)
                    values(("v", c), x1, "Wv")
                if live(s - 7):
                    c = s - 7
                    for i in range(2):
                        pe.wait_ge(p_ready[i], c + 1)
                    for j, n in enumerate(("pta", "ptb")):
                        claim(pe, (n, c))
                        for i in range(4):
                            g = 4 * j + i
                            last = nc.tensor.transpose(bank[plan[(n, c)][0]][:, i * P:i * P + P],
                                                       twice[:, c, g].rearrange("p i m -> p (i m)"), w("ident"))
                        last.then_inc(full((n, c)), 1)
                if live(s - 8):
                    c = s - 8
                    for n in ("v", "pta", "ptb"):
                        evacuated(pe, (n, c))
                    weighted_values(("pv", c), pT)
                if live(s - 9):
                    c = s - 9
                    evacuated(pe, ("pv", c))
                    claim(pe, ("wl", c))
                    mm(ps(("wl", c)), w("Wl"), at[:, c, :], start=True, stop=True).then_inc(full(("wl", c)), 1)
            for c in each:
                if c == BN_AFTER:
                    pe.wait_ge(bn_step, 1)
                    claim(pe, "bn1")
                    mm(ps("bn1", n=2), w("avg"), bn[:, 0:2], start=True, stop=True).then_inc(full("bn1"), 1)
                pe.wait_ge(h01_ready, c + 1)
                claim(pe, ("cen2", c))
                mm(ps(("cen2", c)), w("center"), h01[:, c, :], start=True, stop=False)

            def router_logits(c):
                t = ("lg", c)
                pe.wait_ge(w_loaded[2], 16)
                evacuated(pe, ("cen2", c))
                claim(pe, t)
                for i in range(2 * NT):
                    u, r = i // 2, i % 2
                    last = mm(bank[plan[t][0]][half[r], u * HALVES * NE:(u + 1) * HALVES * NE],
                              x2[:, c, i * TT:i * TT + D], w("router"), start=True, stop=True)
                last.then_inc(full(t), 1)

            for s in range(CHUNKS + 4):
                if live(s):
                    y_wait(pe, s)
                    mm(ps(("cen2", s)), w("center"), hl[:, s, 0:CW], start=False, stop=True).then_inc(full(("cen2", s)), 1)
                if 0 <= s - LG_BEHIND < CHUNKS - 1:
                    router_logits(s - LG_BEHIND)
                if live(s - 1):
                    variance(2, s - 1)

            def one_hot_rows(c):
                pe.wait_ge(oh_ready, c + 1)
                for h in range(HALVES):
                    t = ("oh", c, h)
                    claim(pe, t)
                    for u in range(NT):
                        last = mm(bank[plan[t][0]][half[1], 2 * u * TT:2 * (u + 1) * TT],
                                  onehot[:, c % 2, u, h].rearrange("p i e -> p (i e)"),
                                  ident_b[:, :].rearrange("p (s t) -> p s t", s=2)[:, :, 0:TT], start=True, stop=True)
                    last.then_inc(full(t), 1)

            def hidden(c, i):
                t = ("hid", c, i)
                claim(pe, t)
                mm(ps(t), w1s[:, 0, i % MT, :], xs[:, 0, i // MT, c, :], start=True, stop=False)

            def hidden_own(c, i):
                t = ("hid", c, i)
                mm(ps(t), w1s[:, 1, i % MT, :], xs[:, 1, i // MT, c, :], start=False, stop=True).then_inc(full(t), 1)

            for c in range(CHUNKS + 6):
                if live(c):
                    pe.wait_ge(weights_split, SPLITS1)
                    if c == 0:
                        one_hot_rows(0)
                    pe.wait_ge(split_moved[c], 64)
                    for i in range(AHEAD):
                        hidden(c, i)
                    for h in range(HALVES):
                        evacuated(pe, ("oh", c, h))
                    for i in range(HALVES * MT):
                        if i >= AHEAD:
                            hidden(c, i)
                        hidden_own(c, i)
                        if c == 0 and i == LG_AT:
                            router_logits(CHUNKS - 1)
                        if i == OH_AT and live(c + 1):
                            one_hot_rows(c + 1)
                if live(c - 1):
                    t = ("moe", c - 1)
                    claim(pe, t)
                    for h in range(HALVES):
                        mm(ps(t), b2s[:, h, :], xs[:, 1, h, c - 1, :], start=(h == 0), stop=False)
                    for m in range(MT):
                        for h in range(HALVES):
                            evacuated(pe, ("hid", c - 1, h * MT + m))
                            last = mm(ps(t, half[h]), w("W2", m * D, D), hid[:, (c - 1) % 2, h * MT + m, :],
                               start=False, stop=(m == MT - 1))
                    last.then_inc(full(t), 1)
                if live(c - 2):
                    if c - 2 < CHUNKS - 1:
                        centre_parts(3, c - 2)
                    else:
                        evacuated(pe, ("moe", c - 2))
                        centre(3, h2, c - 2)
                if live(c - 3):
                    variance(3, c - 3)
                for n, behind in (("q1", 6), ("k1", 5)):
                    if live(c - behind):
                        t = (n, c - behind)
                        evacuated(pe, ("cen3", c - behind))
                        claim(pe, t)
                        mm(ps(t), w(n[0] + "w1"), x3[:, c - behind, 0:CW], start=True, stop=True).then_inc(full(t), 1)
                if c == 7:
                    values(("v3", 0), x3, "vw")
            for c in each:
                for n, first_layer, src in (("k2", "k1", k1), ("q2", "q1", q1)):
                    evacuated(pe, (first_layer, c))
                    claim(pe, (n, c))
                    mm(ps((n, c)), w(n[0] + "w2"), src[:, c, 0:CW], start=True, stop=True).then_inc(full((n, c)), 1)
            for c in range(1, CHUNKS):
                values(("v3", c), x3, "vw")
            for s in range(CHUNKS + 4):
                if live(s):
                    pe.wait_ge(kf_ready, s + 1)
                    pe.wait_ge(qf_ready, s + 1)
                    products(("st", s), kf, diag)
                if live(s - 1):
                    evacuated(pe, ("v3", s - 1))
                    evacuated(pe, ("st", s - 1))
                    weighted_values(("ret", s - 1), pT)
                if live(s - 2):
                    evacuated(pe, ("ret", s - 2))
                    centre(4, h3, s - 2)
                if live(s - 3):
                    variance(4, s - 3)
                if live(s - 4):
                    c = s - 4
                    evacuated(pe, ("cen4", c))
                    if c == 0:
                        claim(pe, "gate")
                    for i in range(2 * NT):
                        u, r = i // 2, i % 2
                        at0 = (c * NT + u) * HALVES * EX
                        last = mm(bank[plan["gate"][0]][half[r], at0:at0 + HALVES * EX], x4[:, c, i * TT:i * TT + D],
                                  w("gW"), start=True, stop=True)
                    if c == CHUNKS - 1:
                        last.then_inc(full("gate"), 1)
                    claim(pe, ("s1", c))
                    mm(ps(("s1", c)), w("sW1"), x4[:, c, 0:CW], start=True, stop=True).then_inc(full(("s1", c)), 1)
            for c in each:
                evacuated(pe, ("s1", c))
                for h, n in enumerate(("s2a", "s2b")):
                    claim(pe, (n, c))
                    mm(ps((n, c)), w("sW2", h * P, P), s1[:, c, :], start=True, stop=True).then_inc(full((n, c)), 1)
            for c in range(CHUNKS + 1):
                if c < CHUNKS:
                    pe.wait_ge(weights_split, SPLITS)
                    pe.wait_ge(split_moved[c], 128)
                    for i in range(HALVES * EX):
                        h, x = i // EX, i % EX
                        t = ("e1", c, i)
                        claim(pe, t)
                        mm(ps(t), e1s[:, 0, x, :], xs[:, 0, h, c, :], start=True, stop=False)
                        mm(ps(t), e1s[:, 1, x, :], xs[:, 0, h, c, :], start=False, stop=True).then_inc(full(t), 1)
                        if i == GT_AT:
                            for g in GATES_IN[c]:
                                pe.wait_ge(gp_ready[g * 2 // CHUNKS], 1)
                                t = ("gt", g)
                                claim(pe, t)
                                for u in range(NT):
                                    last = mm(bank[plan[t][0]][:, 2 * u * TT:2 * (u + 1) * TT], gp[:, g, u, :],
                                              ident_r[:, :].rearrange("p (s t) -> p s t", s=2)[:, :, 0:TT],
                                              start=True, stop=True)
                                last.then_inc(full(t), 1)
                if c:
                    evacuated(pe, ("gt", c - 1))
                    for h in range(HALVES):
                        for pair in range(2):
                            i = 2 * h + pair
                            t = ("e2", c - 1, i)
                            claim(pe, t)
                            for j in range(2):
                                x = 2 * pair + j
                                evacuated(pe, ("e1", c - 1, h * EX + x))
                                last = mm(ps(t, half[j]), w("eW2", x * D, D), hid[:, (c - 1) % 2, h * EX + x, :],
                                          start=True, stop=True)
                            last.then_inc(full(t), 1)
                        for pair in range(2):
                            i = 2 * h + pair
                            t = ("g", c - 1, i)
                            claim(pe, t)
                            mm(ps(t), gsel[:, i, :], gT[:, c - 1, :], start=True, stop=True).then_inc(full(t), 1)
                    t = ("fin", c - 1)
                    claim(pe, t)
                    mm(ps(t), b3s[:, :], gT[:, c - 1, :], start=True, stop=False)
                    for h, n in enumerate(("s2a", "s2b")):
                        evacuated(pe, (n, c - 1))
                        mm(ps(t, half[h]), w("sW3"), s2[h][:, c - 1, :], start=False, stop=False)
                    for pair in range(2):
                        for h in range(HALVES):
                            evacuated(pe, ("g", c - 1, 2 * h + pair))
                            last = mm(ps(t, half[h]), w("eW3", pair * D, D), ge[:, (c - 1) % 2, 2 * h + pair, :],
                                      start=False, stop=(pair == 1))
                    last.then_inc(full(t), 1)

        @block.scalar
        def _(act):
            f = nc.scalar.activation

            def square(i, tile, c, bias=0.0):
                arrived(act, (tile, c))
                f(sq[:, c, :], ps((tile, c)), ACT.Square, bias=bias).then_inc(sq_ready[i], 1)

            def log_variance(i, c):
                t = (f"var{i}", c)
                arrived(act, t)
                f(lnv[:, c, :], ps(t), ACT.Ln, bias=eps[:, 0:1]).then_inc(free(t), 1)

            def deviation(i, c):
                evacuated(act, (f"var{i}", c))
                f(rstd[:, c, :], lnv[:, c, :], ACT.Exp, scale=-0.5).then_inc(rstd_ready[i], 1)

            def split_hi(x, tile, c):
                evacuated(act, (tile, c))
                f(xh[:, c, :], x[:, c, 0:CW], ACT.Copy).then_inc(xh_ready, 1)

            act.dma_start(X[:, 0], xblk[:, 0]).then_inc(x_loaded[0], 16)
            act.preload_act_table_set(LN_EXP)
            act.wait_ge(constants, 1)
            evacuated(act, "setup")
            for s in range(CHUNKS + 9):
                if live(s):
                    square(0, "tok", s, tokW[:, 2 * D:2 * D + 1])
                if live(s - 1):
                    log_variance(0, s - 1)
                    deviation(0, s - 1)
                if live(s - 2):
                    square(1, "cen1", s - 2)
                if live(s - 3):
                    log_variance(1, s - 3)
                    deviation(1, s - 3)
                if live(s - 4):
                    c = s - 4
                    act.wait_ge(w_loaded[1], 16)
                    arrived(act, ("q", c))
                    f(q[:, c, 0:CW], ps(("q", c)), ACT.Identity, bias=w("bq")).then_inc(free(("q", c)), 1)
                    act.wait_ge(constants, CONSTANTS)
                    arrived(act, ("k", c))
                    f(diag[half[1], c, :, 1, :], ps(("k", c), half[1]).rearrange("p (b t) -> p b t", t=TOK),
                      ACT.Identity, bias=w("bk", rows=half[1])).then_inc(free(("k", c)), 1)
                if live(s - 5):
                    c = s - 5
                    evacuated(act, ("s", c))
                    f(e[:, c, 0:CW], e[:, c, 0:CW], ACT.Exp, scale=1.0 / D).then_inc(e_ready, 1)
                    arrived(act, ("v", c))
                    f(v[:, c].rearrange("p j h d -> p (j h d)"), ps(("v", c), n=CB * D), ACT.Copy)\
                        .then_inc(free(("v", c)), 1)
                if live(s - 7):
                    c = s - 7
                    arrived(act, ("pta", c))
                    for r in range(2):
                        rows = slice(D * r, D * r + TOK)
                        last = f(pT[rows, c, 0:4, r, :],
                                 bank[plan[("pta", c)][0]][rows, :].rearrange("p (g s n) -> p g s n", s=2, n=D)[:, :, r, 0:TOK],
                                 ACT.Copy)
                    last.then_inc(free(("pta", c)), 1)
                if live(s - 9):
                    c = s - 9
                    act.wait_ge(stats_ready, c + 1)
                    f(hl[:, c, 0:CW], ps(("wl", c)), ACT.Identity, bias=w("bl")).then_inc(free(("wl", c)), 1)
            act.wait_ge(bn_step, 4)
            f(bn[:, 5:6], bank[plan["bn1"][0]][:, 1:2], ACT.Ln, bias=bn[:, 4:5]).then_inc(free("bn1"), 1)
            evacuated(act, "bn1")
            f(bn[:, 6:7], bn[:, 5:6], ACT.Exp, scale=-0.5).then_inc(bn_rstd, 1)
            act.wait_ge(bn_step, 6)
            for c in range(RELU_ACT):
                f(hl[:, c, 0:CW], hl[:, c, 0:CW], ACT.Relu, bias=bn[:, 8:9], scale=bn[:, 7:8]).then_inc(y_ready, 1)

            def route_rows(c):
                for h in range(HALVES):
                    t = ("oh", c, h)
                    arrived(act, t)
                    f(xs[half[1], 1, h, c, :], ps(t, half[1]), ACT.Copy).then_inc(free(t), 1)

            for s in range(CHUNKS + 2):
                if live(s):
                    square(2, "cen2", s)
                if live(s - 1):
                    log_variance(2, s - 1)
                if s == CHUNKS + 1:
                    route_rows(0)
                if live(s - 2):
                    split_hi(x2, "cen2", s - 2)
                if live(s - 1):
                    deviation(2, s - 1)
            for c in range(CHUNKS + 4):
                if 0 <= c - 2 < CHUNKS - 1:
                    evacuated(act, ("moe", c - 2))
                    f(hh[:, c - 2, :], h2[:, c - 2, :], ACT.Copy).then_inc(hh_ready, 1)
                if live(c):
                    if c >= 2:
                        arrived(act, ("moe", c - 2))
                    for i in HID_ACT[c]:
                        t = ("hid", c, i)
                        arrived(act, t)
                        f(hid[:, c % 2, i, :], ps(t), ACT.Relu).then_inc(free(t), 1)
                        if i == OH_AT - 1 and live(c + 1):
                            route_rows(c + 1)
                if live(c - 2):
                    square(3, "cen3", c - 2)
                if live(c - 3):
                    log_variance(3, c - 3)
                    deviation(3, c - 3)
            act.preload_act_table(ACT.Tanh)
            for c in each:
                for n, dst in (("k1", k1), ("q1", q1)):
                    arrived(act, (n, c))
                    f(dst[:, c, 0:CW], ps((n, c)), ACT.Tanh, bias=w(n[0] + "b1")).then_inc(free((n, c)), 1)
            for c in each:
                for n, dst in (("k2", kf), ("q2", qf)):
                    arrived(act, (n, c))
                    f(dst[:, c, 0:CW], ps((n, c)), ACT.Tanh, bias=w(n[0] + "b2")).then_inc(free((n, c)), 1)
            act.preload_act_table(ACT.Sin)
            for c in each:
                act.wait_ge(k_folded, c + 1)
                f(kf[:, c, 0:CW], kf[:, c, 0:CW], ACT.Sin, bias=w("sbias"), scale=PI).then_inc(kf_ready, 1)
                act.wait_ge(q_folded, c + 1)
                for h in range(HALVES):
                    last = f(diag[half[h], c, :, h, :], qf[half[h], c, 0:CW].rearrange("p (b t) -> p b t", t=TOK),
                             ACT.Sin, bias=w("sbias", rows=half[h]), scale=PI)
                last.then_inc(qf_ready, 1)
            act.preload_act_table_set(LN_EXP)
            for s in range(2, CHUNKS + 4):
                if live(s - 2):
                    square(4, "cen4", s - 2)
                if live(s - 3):
                    log_variance(4, s - 3)
                    deviation(4, s - 3)
                if live(s - 4):
                    c = s - 4
                    split_hi(x4, "cen4", c)
                    arrived(act, ("s1", c))
                    f(s1[:, c, :], ps(("s1", c)), ACT.Relu, bias=w("sb1")).then_inc(free(("s1", c)), 1)
            groups = [slice(g * GT // 2, (g + 1) * GT // 2) for g in range(2)]
            for g, rows in enumerate(groups):
                act.wait_ge(gate_step[g], 2)
                f(ga[:, rows], gl[:, rows], ACT.Exp).then_inc(gate_exp[g], 1)
            for c in each:
                if c == EXP2_AT:
                    for g, rows in enumerate(groups):
                        act.wait_ge(gate_step[g], 17)
                        f(gs[:, 5, rows], gs[:, 4, rows], ACT.Exp).then_inc(gate_exp[g], 1)
                for h, n in enumerate(("s2a", "s2b")):
                    arrived(act, (n, c))
                    f(s2[h][:, c, :], ps((n, c)), ACT.Relu, bias=w("sb2")).then_inc(free((n, c)), 1)
            for c in range(CHUNKS + 1):
                if c < CHUNKS:
                    if c >= 2:
                        arrived(act, ("e2", c - 2, 3))
                    for i in E1_ACT[c]:
                        t = ("e1", c, i)
                        arrived(act, t)
                        f(hid[:, c % 2, i, :], ps(t), ACT.Relu, bias=w("eb1", i % EX, 1)).then_inc(free(t), 1)
                        if i == 4 and c == 1:
                            t = ("gt", 0)
                            arrived(act, t)
                            f(gT[:, 0, :], ps(t), ACT.Copy).then_inc(free(t), 1)
                if c:
                    for i in range(4):
                        t = ("e2", c - 1, i)
                        arrived(act, t)
                        if c >= 3:
                            evacuated(act, ("g", c - 3, i))
                        f(e2[:, (c - 1) % 2, i, :], ps(t), ACT.Relu, bias=w("eb2", i % 2, 1)).then_inc(free(t), 1)

        @block.gpsimd
        def _(pool):
            pool.memset(eps[:, :], EPS).then_inc(constants, 1)
            for t in (x1, q, e, x2):
                pool.memset(t[:, :, CW:PADW], 0.0).then_inc(constants, 1)
            pool.memset(twice[:, :, :, :, TOK:D].rearrange("p c g i m -> p (c g i) m"), 0.0).then_inc(constants, 1)
            for t in (diag, pT):
                pool.memset(t[:, :, :, :, :], 0.0).then_inc(constants, 1)
            pool.memset(gp[:, :, :, :].bitcast(F32), 0.0).then_inc(constants, 1)
            for c in each:
                pool.wait_ge(h0_ready, c + 1)
                evacuated(pool, ("cen1", c))
                pool.tensor_tensor(h01[:, c, :], h0[:, c, :], x1[:, c, 0:CW], ALU.add).then_inc(h01_ready, 1)
            for c in each:
                pool.wait_ge(inv_ready, c + 1)
                pool.tensor_tensor(twice[:, c, :, 1, 0:TOK], e[:, c, 0:CW].rearrange("p (g m) -> p g m", m=TOK),
                                   rinv[:, c, :].rearrange("p (g o) -> p g o", o=1).broadcast_to([P, CB, TOK]),
                                   ALU.mult).then_inc(p_ready[1], 1)
            pool.wait_ge(w_loaded[1], 16)
            pool.tensor_copy(ident_b[:, :], w("ident")).then_inc(weights_split, 1)
            pool.wait_ge(w_loaded[2], 16)
            n = 1

            def split_lo(x, c, count):
                pool.wait_ge(xh_ready, count)
                pool.tensor_tensor(xl[:, c, :], x[:, c, 0:CW], xh[:, c, :], ALU.subtract).then_inc(xl_ready[c], 1)

            for name, dst in (("W1", w1s[:, 0].rearrange("p m k -> p (m k)")),
                              ("M1", w1s[:, 1].rearrange("p m k -> p (m k)")),
                              ("B2", b2s[:, :, :].rearrange("p h m -> p (h m)")),
                              ("ident", ident_r), ("center", center_r), ("gsel", gsel), ("eW1", e1s), ("eB3", b3s[:, :])):
                if name == "ident":
                    assert n == SPLITS1
                    for c in each:
                        split_lo(x2, c, c + 1)
                src = w(name)
                if name in ("ident", "center", "gsel"):
                    flat = dst[:, :] if name != "gsel" else dst[:, :, :].rearrange("p i m -> p (i m)")
                    pool.tensor_copy(flat, src).then_inc(weights_split, 1)
                    n += 1
                elif name in ("W1", "M1", "B2", "eB3"):
                    pool.tensor_copy(dst, src).then_inc(weights_split, 1)
                    n += 1
                    for rows in {"W1": (), "M1": (half[0], slice(D + NE, P)), "B2": (slice(D + NE, P),), "eB3": (half[1],)}[name]:
                        pool.wait_ge(weights_split, n)
                        pool.tensor_tensor(dst[rows], w(name, rows=rows), dst[rows], ALU.subtract)\
                            .then_inc(weights_split, 1)
                        n += 1
                else:
                    hi, lo = (dst[:, i].rearrange("p x m -> p (x m)") for i in range(2))
                    pool.tensor_copy(hi, src).then_inc(weights_split, 1)
                    n += 1
                    pool.wait_ge(weights_split, n)
                    pool.tensor_tensor(lo, src, hi, ALU.subtract).then_inc(weights_split, 1)
                    n += 1
                pool.wait_ge(weights_split, n)
            assert n == SPLITS
            for c in range(CHUNKS - 1):
                pool.wait_ge(hh_ready, c + 1)
                pool.tensor_tensor(hlo[:, c, :], h2[:, c, :], hh[:, c, :], ALU.subtract).then_inc(hlo_ready, 1)
            for c in each:
                split_lo(x4, c, CHUNKS + c + 1)

        @block.vector
        def _(dve):
            tt, ts, stt = nc.vector.tensor_tensor, nc.vector.tensor_scalar, nc.vector.scalar_tensor_tensor

            def across(column, n):
                return column.rearrange("p (g o) -> p g o", o=1).broadcast_to([column.shape[0], column.shape[1], n])

            def normalise(i, dst, c):
                dve.wait_ge(rstd_ready[i], c + 1)
                t = (f"cen{i}", c)
                tt(dst[:, c, 0:CW], ps(t), rstd[:, c, :], ALU.mult).then_inc(free(t), 1)

            arrived(dve, "setup")
            nc.vector.tensor_copy(tokW[:, :], bank[0][:, 0:2 * D + 1]).then_inc(free("setup"), 1)
            evacuated(dve, "setup")
            for s in range(CHUNKS + 10):
                if live(s - 1):
                    c = s - 1
                    dve.wait_ge(rstd_ready[0], c + 1)
                    t = ("tok", c)
                    stt(out=z[:, c, :], in0=ps(t), scalar=tokW[:, 2 * D:2 * D + 1], in1=rstd[:, c, :],
                        op0=ALU.add, op1=ALU.mult).then_inc(free(t), 1)
                    evacuated(dve, t)
                    ts(h0[:, c, :], z[:, c, :], w("tokg"), w("tokbeta"), ALU.mult, ALU.add).then_inc(h0_ready, 1)
                if live(s - 3):
                    normalise(1, x1, s - 3)
                if live(s - 4):
                    c = s - 4
                    dve.wait_ge(w_loaded[1], 16)
                    dve.wait_ge(constants, CONSTANTS)
                    arrived(dve, ("k", c))
                    ts(diag[half[0], c, :, 0, :], ps(("k", c), half[0]).rearrange("p (b t) -> p b t", t=TOK),
                       w("bk", rows=half[0]), None, ALU.add).then_inc(free(("k", c)), 1)
                if live(s - 5):
                    c = s - 5
                    arrived(dve, ("s", c))
                    scores = ps(("s", c)).rearrange("p (b m) -> p b m", b=CB)
                    nc.vector.reduce_max(mx[:, c, :], scores, AX.X).then_inc(max_ready, 1)
                    dve.wait_ge(max_ready, c + 1)
                    tt(e[:, c, 0:CW].rearrange("p (b m) -> p b m", b=CB), scores, across(mx[:, c, :], TOK),
                       ALU.subtract).then_inc(free(("s", c)), 1)
                if live(s - 6):
                    c = s - 6
                    ec = e[:, c, 0:CW].rearrange("p (b m) -> p b m", b=CB)
                    dve.wait_ge(e_ready, c + 1)
                    nc.vector.reduce_sum(rsum[:, c, :], ec, AX.X).then_inc(sum_ready, 1)
                    dve.wait_ge(sum_ready, c + 1)
                    nc.vector.reciprocal(rinv[:, c, :], rsum[:, c, :]).then_inc(inv_ready, 1)
                    dve.wait_ge(inv_ready, c + 1)
                    tt(twice[:, c, :, 0, 0:TOK], ec, across(rinv[:, c, :], TOK), ALU.mult).then_inc(p_ready[0], 1)
                if live(s - 7):
                    c = s - 7
                    arrived(dve, ("ptb", c))
                    for r in range(2):
                        rows = slice(D * r, D * r + TOK)
                        last = nc.vector.tensor_copy(
                            pT[rows, c, 4:8, r, :],
                            bank[plan[("ptb", c)][0]][rows, :].rearrange("p (g s n) -> p g s n", s=2, n=D)[:, :, r, 0:TOK])
                    last.then_inc(free(("ptb", c)), 1)
                if live(s - 8):
                    c = s - 8
                    arrived(dve, ("pv", c))
                    ts(at[:, c, :], ps(("pv", c)), w("bv"), None, ALU.add).then_inc(free(("pv", c)), 1)
                if live(s - 9):
                    c = s - 9
                    arrived(dve, ("wl", c))
                    nc.vector.bn_stats(stats[:, c, :], ps(("wl", c))).then_inc(stats_ready, 1)
            dve.wait_ge(stats_ready, CHUNKS)
            nc.vector.bn_aggr(bn[:, 0:2], stats[:, :, :]).then_inc(bn_step, 1)
            arrived(dve, "bn1")
            mean = bank[plan["bn1"][0]][:, 0:1]
            tt(bn[:, 3:4], bn[:, 0:1], mean, ALU.subtract).then_inc(bn_step, 1)
            stt(out=bn[:, 2:3], in0=mean, scalar=-1.0, in1=w("bl"), op0=ALU.mult, op1=ALU.subtract).then_inc(bn_step, 1)
            dve.wait_ge(bn_step, 2)
            stt(out=bn[:, 4:5], in0=bn[:, 3:4], scalar=bn[:, 3:4], in1=eps[:, 0:1], op0=ALU.mult, op1=ALU.add)\
                .then_inc(bn_step, 1)
            dve.wait_ge(bn_rstd, 1)
            tt(bn[:, 7:8], bn[:, 6:7], w("bng"), ALU.mult).then_inc(bn_step, 1)
            dve.wait_ge(bn_step, 5)
            stt(out=bn[:, 8:9], in0=bn[:, 2:3], scalar=bn[:, 7:8], in1=w("bnb"), op0=ALU.mult, op1=ALU.add)\
                .then_inc(bn_step, 1)
            dve.wait_ge(bn_step, 6)
            for c in range(RELU_ACT, CHUNKS):
                evacuated(dve, ("wl", c))
                ts(hl[:, c, 0:CW], hl[:, c, 0:CW], bn[:, 7:8], bn[:, 8:9], ALU.mult, ALU.add).then_inc(y_step, 1)
            for c in range(RELU_ACT, CHUNKS):
                dve.wait_ge(y_step, c - RELU_ACT + 1)
                ts(hl[:, c, 0:CW], hl[:, c, 0:CW], 0.0, None, ALU.max).then_inc(y2_ready, 1)
            for c in each:
                y_wait(dve, c)
                dve.wait_ge(h01_ready, c + 1)
                tt(h1[:, c, :], h01[:, c, :], hl[:, c, 0:CW], ALU.add).then_inc(h1_ready, 1)

            def logits(c):
                t = ("lg", c)
                arrived(dve, t)
                tt(lg[:, c].rearrange("p (u h) e -> p u (h e)", u=NT),
                   ps(t, n=NT * HALVES * NE).rearrange("p (u g) -> p u g", u=NT),
                   w("routerb").rearrange("p (o g) -> p o g", o=1).broadcast_to([P, NT, HALVES * NE]),
                   ALU.add).then_inc(free(t), 1)

            def largest(c):
                evacuated(dve, ("lg", c))
                nc.vector.reduce_max(lmx[:, c, :], lg[:, c], AX.X).then_inc(route_step[c], 1)

            def mark(c):
                dve.wait_ge(route_step[c], 1)
                tt(first[:, c], lg[:, c], across(lmx[:, c, :], NE), ALU.is_equal).then_inc(route_step[c], 1)

            def rank_marks(c):
                dve.wait_ge(route_step[c], 2)
                by_tile = first[:, c].rearrange("p (u h) e -> p u (h e)", u=NT)
                tt(by_tile, by_tile, w("rank").rearrange("p (o g) -> p o g", o=1).broadcast_to([P, NT, HALVES * NE]),
                   ALU.mult).then_inc(route_step[c], 1)

            def first_rank(c):
                dve.wait_ge(route_step[c], 3)
                nc.vector.reduce_max(lmx[:, c, :], first[:, c], AX.X).then_inc(route_step[c], 1)

            def one_hot(c):
                dve.wait_ge(route_step[c], 4)
                if c >= 2:
                    arrived(dve, ("oh", c - 2, 1))
                groups = NT * HALVES
                tt(onehot[:, c % 2].rearrange("p u h i e -> p (u h) i e"),
                   first[:, c].rearrange("p g (i e) -> p g i e", i=1).broadcast_to([P, groups, 2, NE]),
                   lmx[:, c, :].rearrange("p (g i e) -> p g i e", i=1, e=1).broadcast_to([P, groups, 2, NE]),
                   ALU.is_equal).then_inc(oh_ready, 1)

            normalise(2, x2, 0)
            logits(0)
            largest(0)
            normalise(2, x2, 1)
            mark(0)
            rank_marks(0)
            first_rank(0)
            normalise(2, x2, 2)
            one_hot(0)
            logits(1)
            largest(1)
            normalise(2, x2, 3)
            mark(1)
            logits(2)
            rank_marks(1)
            largest(2)
            first_rank(1)
            logits(3)
            one_hot(1)
            mark(2)
            largest(3)
            rank_marks(2)
            mark(3)
            first_rank(2)
            rank_marks(3)
            one_hot(2)
            first_rank(3)
            for c in range(CHUNKS + 4):
                if live(c):
                    if c >= 2:
                        arrived(dve, ("moe", c - 2))
                    for i in sorted(set(range(HALVES * MT)) - set(HID_ACT[c])):
                        t = ("hid", c, i)
                        arrived(dve, t)
                        ts(hid[:, c % 2, i, :], ps(t), 0.0, None, ALU.max).then_inc(free(t), 1)
                    if c == 0:
                        one_hot(3)
                if live(c - 1):
                    t = ("moe", c - 1)
                    arrived(dve, t)
                    stt(out=h2[:, c - 1, :], in0=ps(t), scalar=0.0, in1=h1[:, c - 1, :],
                        op0=ALU.max, op1=ALU.add).then_inc(free(t), 1)
                if live(c - 3):
                    normalise(3, x3, c - 3)

            def layer1_values(c):
                t = ("v3", c)
                arrived(dve, t)
                tt(v[:, c].rearrange("p j h d -> p (j h d)"), ps(t, n=CB * D), w("vb"), ALU.add).then_inc(free(t), 1)

            layer1_values(0)
            for c in each:
                for n, folded, dst in (("k2", k_folded, kf), ("q2", q_folded, qf)):
                    evacuated(dve, (n, c))
                    stt(out=dst[:, c, 0:CW], in0=dst[:, c, 0:CW], scalar=w("fold"), in1=dst[:, c, 0:CW],
                        op0=ALU.mult, op1=ALU.min).then_inc(folded, 1)
            for c in range(1, CHUNKS):
                layer1_values(c)
            for s in range(CHUNKS + 4):
                if live(s):
                    t = ("st", s)
                    arrived(dve, t)
                    for r in range(2):
                        rows = slice(D * r, D * r + TOK)
                        last = tt(pT[rows, s, :, r, :], ps(t, rows).rearrange("p (g n) -> p g n", n=TOK),
                                  w("causal", rows=rows).rearrange("p (o n) -> p o n", o=1).broadcast_to([TOK, CB, TOK]),
                                  ALU.mult)
                    last.then_inc(free(t), 1)
                if live(s - 1):
                    t = ("ret", s - 1)
                    arrived(dve, t)
                    tt(h3[:, s - 1, :], ps(t), h2[:, s - 1, :], ALU.add).then_inc(free(t), 1)
                if live(s - 3):
                    normalise(4, x4, s - 3)
            arrived(dve, "gate")
            G = slice(0, P)
            tt(gl[G].rearrange("p (t h) e -> p t (h e)", h=HALVES),
               ps("gate", G, GT * EX).rearrange("p (t g) -> p t g", g=HALVES * EX),
               w("gb", rows=G).rearrange("p (o g) -> p o g", o=1).broadcast_to([P, GT // HALVES, HALVES * EX]),
               ALU.add).then_inc(free("gate"), 1)
            evacuated(dve, "gate")

            def gate_parts(g, rows):
                gates = gsum[:, rows].rearrange("p (t r h) e -> p t r (h e)", r=1, h=HALVES)
                parts = gp[:, :, :, :].rearrange("p c u (r k g) -> p (c u) r k g", r=2, g=HALVES * EX)
                tiles = slice(g * GT // 4, (g + 1) * GT // 4)
                return (gates.broadcast_to([P, GT // 4, 2, HALVES * EX]), parts[:, tiles, :, 0, :], parts[:, tiles, :, 1, :])

            groups = [slice(g * GT // 2, (g + 1) * GT // 2) for g in range(2)]
            rank = w("grank", 0, EX, G).rearrange("p (o e) -> p o e", o=1).broadcast_to([P, GT // 2, EX])
            for g, rows in enumerate(groups):
                nc.vector.reduce_max(gs[G, 0, rows], gl[G, rows], AX.X).then_inc(gate_step[g], 1)
            for g, rows in enumerate(groups):
                dve.wait_ge(gate_step[g], 1)
                tt(gl[G, rows], gl[G, rows], across(gs[G, 0, rows], EX), ALU.subtract).then_inc(gate_step[g], 1)
            for g, rows in enumerate(groups):
                dve.wait_ge(gate_exp[g], 1)
                nc.vector.reduce_sum(gs[G, 1, rows], ga[G, rows], AX.X).then_inc(gate_step[g], 1)
            for g, rows in enumerate(groups):
                dve.wait_ge(gate_step[g], 3)
                nc.vector.reciprocal(gs[G, 2, rows], gs[G, 1, rows]).then_inc(gate_step[g], 1)
            for g, rows in enumerate(groups):
                dve.wait_ge(gate_step[g], 4)
                tt(ga[G, rows], ga[G, rows], across(gs[G, 2, rows], EX), ALU.mult).then_inc(gate_step[g], 1)
            for g, rows in enumerate(groups):
                dve.wait_ge(gate_step[g], 5)
                nc.vector.reduce_max(gs[G, 0, rows], ga[G, rows], AX.X).then_inc(gate_step[g], 1)
            for g, rows in enumerate(groups):
                dve.wait_ge(gate_step[g], 6)
                tt(gc[G, rows], ga[G, rows], across(gs[G, 0, rows], EX), ALU.is_equal).then_inc(gate_step[g], 1)
            for g, rows in enumerate(groups):
                dve.wait_ge(gate_step[g], 7)
                tt(gc[G, rows], gc[G, rows], rank, ALU.mult).then_inc(gate_step[g], 1)
            for g, rows in enumerate(groups):
                dve.wait_ge(gate_step[g], 8)
                nc.vector.reduce_max(gs[G, 3, rows], gc[G, rows], AX.X).then_inc(gate_step[g], 1)
            for g, rows in enumerate(groups):
                dve.wait_ge(gate_step[g], 9)
                tt(gm1[G, rows], gc[G, rows], across(gs[G, 3, rows], EX), ALU.is_equal).then_inc(gate_step[g], 1)
            for g, rows in enumerate(groups):
                dve.wait_ge(gate_step[g], 10)
                stt(out=gl[G, rows], in0=gm1[G, rows], scalar=-2.0, in1=ga[G, rows], op0=ALU.mult, op1=ALU.add).then_inc(gate_step[g], 1)
            for g, rows in enumerate(groups):
                dve.wait_ge(gate_step[g], 11)
                nc.vector.reduce_max(gs[G, 1, rows], gl[G, rows], AX.X).then_inc(gate_step[g], 1)
            for g, rows in enumerate(groups):
                dve.wait_ge(gate_step[g], 12)
                tt(gc[G, rows], gl[G, rows], across(gs[G, 1, rows], EX), ALU.is_equal).then_inc(gate_step[g], 1)
            for g, rows in enumerate(groups):
                dve.wait_ge(gate_step[g], 13)
                tt(gc[G, rows], gc[G, rows], rank, ALU.mult).then_inc(gate_step[g], 1)
            for g, rows in enumerate(groups):
                dve.wait_ge(gate_step[g], 14)
                nc.vector.reduce_max(gs[G, 3, rows], gc[G, rows], AX.X).then_inc(gate_step[g], 1)
            for g, rows in enumerate(groups):
                dve.wait_ge(gate_step[g], 15)
                tt(gm2[G, rows], gc[G, rows], across(gs[G, 3, rows], EX), ALU.is_equal).then_inc(gate_step[g], 1)
                tt(gs[G, 4, rows], gs[G, 1, rows], gs[G, 0, rows], ALU.subtract).then_inc(gate_step[g], 1)
            for g, rows in enumerate(groups):
                dve.wait_ge(gate_exp[g], 2)
                ts(gs[G, 6, rows], gs[G, 5, rows], 1.0, None, ALU.add).then_inc(gate_step[g], 1)
            for g, rows in enumerate(groups):
                dve.wait_ge(gate_step[g], 18)
                nc.vector.reciprocal(gs[G, 2, rows], gs[G, 6, rows]).then_inc(gate_step[g], 1)
            for g, rows in enumerate(groups):
                dve.wait_ge(gate_step[g], 19)
                tt(gs[G, 7, rows], gs[G, 5, rows], gs[G, 2, rows], ALU.mult).then_inc(gate_step[g], 1)
                tt(gm1[G, rows], gm1[G, rows], across(gs[G, 2, rows], EX), ALU.mult).then_inc(gate_step[g], 1)
            for g, rows in enumerate(groups):
                dve.wait_ge(gate_step[g], 20)
                tt(gm2[G, rows], gm2[G, rows], across(gs[G, 7, rows], EX), ALU.mult).then_inc(gate_step[g], 1)
            for g, rows in enumerate(groups):
                dve.wait_ge(gate_step[g], 22)
                tt(gsum[G, rows], gm1[G, rows], gm2[G, rows], ALU.add).then_inc(gate_step[g], 1)
            for g, rows in enumerate(groups):
                dve.wait_ge(gate_step[g], 23)
                gates, hi, _ = gate_parts(g, rows)
                nc.vector.tensor_copy(hi, gates).then_inc(gate_step[g], 1)
            for g, rows in enumerate(groups):
                dve.wait_ge(gate_step[g], 24)
                gates, hi, lo = gate_parts(g, rows)
                tt(lo, gates, hi, ALU.subtract).then_inc(gp_ready[g], 1)
            for c in range(CHUNKS + 1):
                if c < CHUNKS:
                    if c >= 2:
                        arrived(dve, ("e2", c - 2, 3))
                    for i in range(HALVES * EX):
                        if i not in E1_ACT[c]:
                            t = ("e1", c, i)
                            arrived(dve, t)
                            ts(hid[:, c % 2, i, :], ps(t), w("eb1", i % EX, 1), 0.0, ALU.add, ALU.max)\
                                .then_inc(free(t), 1)
                        if i == 5 and c:
                            t = ("gt", c)
                            arrived(dve, t)
                            nc.vector.tensor_copy(gT[:, c, :], ps(t)).then_inc(free(t), 1)
                if c:
                    for i in range(4):
                        t = ("g", c - 1, i)
                        arrived(dve, t)
                        evacuated(dve, ("e2", c - 1, i))
                        tt(ge[:, (c - 1) % 2, i, :], ps(t), e2[:, (c - 1) % 2, i, :], ALU.mult).then_inc(free(t), 1)
                    t = ("fin", c - 1)
                    arrived(dve, t)
                    stt(out=res[:, c - 1, :], in0=ps(t), scalar=w("sb3"), in1=h3[:, c - 1, :],
                        op0=ALU.add, op1=ALU.add).then_inc(free(t), 1)


def pack_weights(a):
    pack = np.zeros((P, PACKW), np.float32)

    def put(name, block, row=0, lo=0):
        pack[row:row + block.shape[0], COL[name] + lo:COL[name] + lo + block.shape[1]] = block

    def both(name, block):
        for h in range(HALVES):
            put(name, block, D * h, block.shape[1] * h)

    def column(name, vec, lo=0):
        for r in range(0, P, len(vec)):
            put(name, vec[:, None], r, lo)

    eye = np.eye(D, dtype=np.float32)
    ones = np.ones((D, D), np.float32)
    for i in range(2):
        put("tokW", a["L0_tok_W"][:, i * P:i * P + P], D * i)
    both("center", eye - np.float32(1.0 / D) * ones)
    both("mean", np.float32(1.0 / D) * ones)
    column("tokb", a["L0_tok_b"])
    column("tokg", a["L0_tok_gamma"])
    column("tokbeta", a["L0_tok_beta"])
    for n in "qkvl":
        both("W" + n, a["L0_attn_W" + n])
        column("b" + n, a["L0_attn_b" + n])
    column("bng", a["L0_attn_gamma"])
    column("bnb", a["L0_attn_beta"])
    pack[:, COL["avg"]:COL["avg"] + P] = np.tile(np.float32(0.5) * eye, (2, 2))
    put("ident", np.eye(P, dtype=np.float32))
    both("router", a["L0_ffn_router_w"].T)
    put("routerb", np.tile(a["L0_ffn_router_b"], (P, HALVES)))
    put("rank", np.tile(np.arange(NE, 0, -1, dtype=np.float32), (P, HALVES)))
    w1 = a["L0_ffn_W1"].transpose(1, 0, 2).reshape(D, NE * NH)
    own = np.full((NE, NE, NH), -BIG, np.float32)
    own[np.arange(NE), np.arange(NE)] = a["L0_ffn_b1"]
    w2 = a["L0_ffn_W2"].reshape(NE * NH, D)
    put("M1", w1)
    for h in range(HALVES):
        put("W1", w1, D * h)
        for r in (D, D + NE):
            put("B2", a["L0_ffn_b2"], r, h * P + h * D)
    for r in (D, D + NE):
        put("M1", own.reshape(NE, NE * NH), r)
    for m in range(MT):
        put("W2", w2[m * P:m * P + P], 0, m * D)
    for n in "kq":
        both(n + "w1", a[f"L1_attn_{n}w1"].T)
        both(n + "w2", np.tile(a[f"L1_attn_{n}w2"].T, (1, 2)))
        column(n + "b1", a[f"L1_attn_{n}b1"])
        column(n + "b2", a[f"L1_attn_{n}b2"])
    both("vw", a["L1_attn_vw"].T)
    put("vb", np.tile(a["L1_attn_vb"], (P, CB)))
    m, n = np.arange(P)[:, None] % D, np.arange(TOK)[None]
    put("causal", np.where(m <= n, 1.0 / np.sqrt((n + 1.0) * KP), 0.0).astype(np.float32))
    cosine = (np.arange(P) % D < KP)
    column("fold", np.where(cosine, -1.0, 1.0).astype(np.float32))
    column("sbias", np.where(cosine, np.pi / 2, 0.0).astype(np.float32))
    both("gW", a["L1_ffn_gW"])
    put("gb", np.tile(a["L1_ffn_gb"], (P, HALVES)))
    put("grank", np.tile(np.arange(EX, 0, -1, dtype=np.float32), (P, HALVES)))
    both("sW1", a["L1_ffn_sW1"])
    put("sW3", a["L1_ffn_sW3"])
    column("sb1", a["L1_ffn_sb1"])
    column("sb2", a["L1_ffn_sb2"])
    column("sb3", a["L1_ffn_sb3"])
    for h in range(HALVES):
        put("sW2", a["L1_ffn_sW2"], D * h, h * P)
        for x in range(EX):
            put("eW1", a["L1_ffn_eW1"][x], D * h, x * P)
            pair, j = x // 2, x % 2
            for r in (0, HALVES * EX):
                put("gsel", np.ones((1, D), np.float32), r + h * EX + x, (2 * h + pair) * P + j * D)
        for r in (0, HALVES * EX, D, D + HALVES * EX):
            put("eB3", a["L1_ffn_eb3"], r + EX * h, h * D)
    for x in range(EX):
        put("eW2", a["L1_ffn_eW2"][x], 0, x * D)
        put("eW3", a["L1_ffn_eW3"][x], D * (x % 2), (x // 2) * D)
        column("eb1", a["L1_ffn_eb1"][x], x)
        put("eb2", a["L1_ffn_eb2"][x][:, None], D * (x % 2), x // 2)
    return pack


def kernel(**inputs):
    import concourse.bacc as bacc
    from concourse.bass_utils import run_bass_kernel_spmd

    a = {n: np.asarray(x) for n, x in inputs.items()}
    x = a["x"][:, :BLOCKS * STRIDE].reshape(HALVES, CHUNKS, CB, BLOCKS, STRIDE * FEAT)
    arrays = {"xblk": np.ascontiguousarray(x.transpose(4, 1, 0, 2, 3)), "wpack": pack_weights(a)}
    nc = bacc.Bacc("TRN2", target_bir_lowering=False, num_devices=1)
    args = [nc.dram_tensor(n, v.shape, F32, kind="ExternalInput").ap() for n, v in arrays.items()]
    out = nc.dram_tensor("out", (P, CHUNKS, CW), F32, kind="ExternalOutput").ap()
    audio_tower_kernel(nc, *args, out)
    r = run_bass_kernel_spmd(nc, [arrays], core_ids=[0])
    o = r.results[0]["out"].reshape(HALVES, D, CHUNKS, CB, TOK)
    return np.ascontiguousarray(o.transpose(0, 2, 3, 4, 1)).reshape(B, TOK, D)
```
